# Optimizing a Trainium2 kernel written in Bass

```python
import numpy as np
import jax
import jax.numpy as jnp

def _softmax(x, axis=-1):
    return jax.nn.softmax(x, axis=axis)

def _gelu(x):
    return jax.nn.gelu(x, approximate=True)

def _silu(x):
    return jax.nn.silu(x)

def _sigmoid(x):
    return jax.nn.sigmoid(x)

def _layernorm(x, axis=-1, eps=1e-05):
    m = jnp.mean(x, axis=axis, keepdims=True)
    v = jnp.var(x, axis=axis, keepdims=True)
    return (x - m) / jnp.sqrt(v + eps)

def _scatter_add(tgt, idx, src, axis=0):
    return tgt.at[idx].add(src)

def _segment_sum(src, seg, n):
    return jax.ops.segment_sum(src, seg, n)
kernel_name = 'mk_xattn_seq_d1_seqx_r2_027cd3'

def setup_inputs(seed: int=0):
    np.random.seed(seed)
    _w = jnp.asarray

    def _rec_inputs():
        import jax
        import jax.numpy as jnp
        _rk = jax.random.key(seed)
        x = -0.0001951 + 1 * jax.random.normal(jax.random.fold_in(_rk, 1), (8, 224, 512), jnp.float32)
        _lenS = 224 - jax.random.randint(jax.random.fold_in(_rk, 7), (8,), 0, max(1, 224 // 4) + 1, jnp.int32)
        _lenS2 = 750 - jax.random.randint(jax.random.fold_in(_rk, 8), (8,), 0, max(1, 750 // 4) + 1, jnp.int32)
        _ctx_1024P = jax.random.normal(jax.random.fold_in(_rk, 11), (8, 16, 512), jnp.float32)
        _ctx_1024c = jax.random.dirichlet(jax.random.fold_in(_rk, 511), 0.3 * jnp.ones((16,), jnp.float32), (8, 750))
        _ctx_1024t = jnp.einsum('bsk,bkd->bsd', _ctx_1024c, _ctx_1024P)
        _ctx_1024t = _ctx_1024t * jax.lax.rsqrt(jnp.mean(jnp.square(_ctx_1024t)) + 1e-12) * 0.953939
        ctx_1024 = -4.82715e-05 + 0.999928 * (_ctx_1024t + 0.3 * jax.random.normal(jax.random.fold_in(_rk, 611), (8, 750, 512), jnp.float32))
        _validS = jnp.arange(224)[None, :] < _lenS[:, None]
        _validS2 = jnp.arange(750)[None, :] < _lenS2[:, None]
        _causal = jnp.tril(jnp.ones((224, 224), dtype=bool))
        mask_BxS_bf0 = jnp.logical_not(jnp.ones((8, 224), dtype=bool))
        return (x, ctx_1024, mask_BxS_bf0)
    x, ctx_1024, mask_BxS_bf0 = _rec_inputs()

    def _L0_xattn_setup():
        import jax, jax.numpy as jnp
        import numpy as np
        B, T, J, C, H = (16, 224, 224, 512, 16)
        HD = C // H
        NEG_INF = float('-inf')

        def _layernorm(x, g, b, eps=1e-05):
            mu = jnp.mean(x, axis=-1, keepdims=True)
            var = jnp.var(x, axis=-1, keepdims=True)
            return (x - mu) * jax.lax.rsqrt(var + eps) * g + b

        def _heads(x):
            Bv, S, _ = x.shape
            return x.reshape(Bv, S, H, HD).transpose(0, 2, 1, 3)

        def _merge(x):
            Bv, _, S, _ = x.shape
            return x.transpose(0, 2, 1, 3).reshape(Bv, S, C)

        def _forward(tgt, src, sa_wqkv, sa_wproj, sa_bproj, ed_wkv, ed_wq, ed_wproj, ed_bproj, ff_w1, ff_b1, ff_w2, ff_b2, ln1_g, ln1_b, ln2_g, ln2_b, ln3_g, ln3_b, tgt_padding_mask):
            scale = C ** (-0.5)
            x = _layernorm(tgt, ln1_g, ln1_b)
            qkv = x @ sa_wqkv
            q, k, v = (_heads(t) for t in jnp.split(qkv, 3, axis=-1))
            wei = jnp.einsum('bhtd,bhsd->bhts', q, k) * scale
            causal = jnp.tril(jnp.ones((T, T), bool))
            wei = jnp.where(causal[None, None], wei, NEG_INF)
            wei = jnp.where(tgt_padding_mask[:, None, None, :], NEG_INF, wei)
            wei = jax.nn.softmax(wei, axis=-1)
            sa_out = _merge(jnp.einsum('bhts,bhsd->bhtd', wei, v)) @ sa_wproj + sa_bproj
            result = tgt + sa_out
            xq = _layernorm(result, ln2_g, ln2_b)
            xs = _layernorm(src, ln2_g, ln2_b)
            kv = xs @ ed_wkv
            k2, v2 = (_heads(t) for t in jnp.split(kv, 2, axis=-1))
            q2 = _heads(xq @ ed_wq)
            wei2 = jnp.einsum('bhtd,bhjd->bhtj', q2, k2) * scale
            wei2 = jax.nn.softmax(wei2, axis=-1)
            ed_out = _merge(jnp.einsum('bhtj,bhjd->bhtd', wei2, v2)) @ ed_wproj + ed_bproj
            result = result + ed_out
            h = jax.nn.relu(_layernorm(tgt, ln3_g, ln3_b) @ ff_w1 + ff_b1)
            result = result + (h @ ff_w2 + ff_b2)
            return result
        key = jax.random.key(seed)
        ks = jax.random.split(key, 16)
        s = 0.02
        return {'tgt': jax.random.normal(ks[0], (B, T, C), jnp.float32), 'src': jax.random.normal(ks[1], (B, J, C), jnp.float32), 'sa_wqkv': jax.random.normal(ks[2], (C, 3 * C), jnp.float32) * s, 'sa_wproj': jax.random.normal(ks[3], (C, C), jnp.float32) * s, 'sa_bproj': jnp.zeros((C,), jnp.float32), 'ed_wkv': jax.random.normal(ks[4], (C, 2 * C), jnp.float32) * s, 'ed_wq': jax.random.normal(ks[5], (C, C), jnp.float32) * s, 'ed_wproj': jax.random.normal(ks[6], (C, C), jnp.float32) * s, 'ed_bproj': jnp.zeros((C,), jnp.float32), 'ff_w1': jax.random.normal(ks[7], (C, 4 * C), jnp.float32) * s, 'ff_b1': jnp.zeros((4 * C,), jnp.float32), 'ff_w2': jax.random.normal(ks[8], (4 * C, C), jnp.float32) * s, 'ff_b2': jnp.zeros((C,), jnp.float32), 'ln1_g': jnp.ones((C,), jnp.float32), 'ln1_b': jnp.zeros((C,), jnp.float32), 'ln2_g': jnp.ones((C,), jnp.float32), 'ln2_b': jnp.zeros((C,), jnp.float32), 'ln3_g': jnp.ones((C,), jnp.float32), 'ln3_b': jnp.zeros((C,), jnp.float32), 'tgt_padding_mask': jnp.zeros((B, T), bool)}
    _L0_xattn_all = _L0_xattn_setup()
    _L0_xattn_in = {k: v for k, v in _L0_xattn_all.items() if k in ('sa_wqkv', 'sa_wproj', 'sa_bproj', 'ed_wkv', 'ed_wq', 'ed_wproj', 'ed_bproj', 'ff_w1', 'ff_b1', 'ff_w2', 'ff_b2', 'ln1_g', 'ln1_b', 'ln2_g', 'ln2_b', 'ln3_g', 'ln3_b')}
    del _L0_xattn_all
    return {'x': x, 'ctx_1024': ctx_1024, 'mask_BxS_bf0': mask_BxS_bf0, 'L0_xattn_sa_wqkv': _L0_xattn_in['sa_wqkv'], 'L0_xattn_sa_wproj': _L0_xattn_in['sa_wproj'], 'L0_xattn_sa_bproj': _L0_xattn_in['sa_bproj'], 'L0_xattn_ed_wkv': _L0_xattn_in['ed_wkv'], 'L0_xattn_ed_wq': _L0_xattn_in['ed_wq'], 'L0_xattn_ed_wproj': _L0_xattn_in['ed_wproj'], 'L0_xattn_ed_bproj': _L0_xattn_in['ed_bproj'], 'L0_xattn_ff_w1': _L0_xattn_in['ff_w1'], 'L0_xattn_ff_b1': _L0_xattn_in['ff_b1'], 'L0_xattn_ff_w2': _L0_xattn_in['ff_w2'], 'L0_xattn_ff_b2': _L0_xattn_in['ff_b2'], 'L0_xattn_ln1_g': _L0_xattn_in['ln1_g'], 'L0_xattn_ln1_b': _L0_xattn_in['ln1_b'], 'L0_xattn_ln2_g': _L0_xattn_in['ln2_g'], 'L0_xattn_ln2_b': _L0_xattn_in['ln2_b'], 'L0_xattn_ln3_g': _L0_xattn_in['ln3_g'], 'L0_xattn_ln3_b': _L0_xattn_in['ln3_b']}

def reference(x, ctx_1024, mask_BxS_bf0, L0_xattn_sa_wqkv, L0_xattn_sa_wproj, L0_xattn_sa_bproj, L0_xattn_ed_wkv, L0_xattn_ed_wq, L0_xattn_ed_wproj, L0_xattn_ed_bproj, L0_xattn_ff_w1, L0_xattn_ff_b1, L0_xattn_ff_w2, L0_xattn_ff_b2, L0_xattn_ln1_g, L0_xattn_ln1_b, L0_xattn_ln2_g, L0_xattn_ln2_b, L0_xattn_ln3_g, L0_xattn_ln3_b):
    import jax
    import jax.numpy as jnp

    def _L0_xattn_ref(tgt, src, sa_wqkv, sa_wproj, sa_bproj, ed_wkv, ed_wq, ed_wproj, ed_bproj, ff_w1, ff_b1, ff_w2, ff_b2, ln1_g, ln1_b, ln2_g, ln2_b, ln3_g, ln3_b, tgt_padding_mask):
        import jax, jax.numpy as jnp
        import numpy as np
        B, T, J, C, H = (16, 224, 224, 512, 16)
        HD = C // H
        NEG_INF = float('-inf')

        def _layernorm(x, g, b, eps=1e-05):
            mu = jnp.mean(x, axis=-1, keepdims=True)
            var = jnp.var(x, axis=-1, keepdims=True)
            return (x - mu) * jax.lax.rsqrt(var + eps) * g + b

        def _heads(x):
            Bv, S, _ = x.shape
            return x.reshape(Bv, S, H, HD).transpose(0, 2, 1, 3)

        def _merge(x):
            Bv, _, S, _ = x.shape
            return x.transpose(0, 2, 1, 3).reshape(Bv, S, C)

        def _forward(tgt, src, sa_wqkv, sa_wproj, sa_bproj, ed_wkv, ed_wq, ed_wproj, ed_bproj, ff_w1, ff_b1, ff_w2, ff_b2, ln1_g, ln1_b, ln2_g, ln2_b, ln3_g, ln3_b, tgt_padding_mask):
            scale = C ** (-0.5)
            x = _layernorm(tgt, ln1_g, ln1_b)
            qkv = x @ sa_wqkv
            q, k, v = (_heads(t) for t in jnp.split(qkv, 3, axis=-1))
            wei = jnp.einsum('bhtd,bhsd->bhts', q, k) * scale
            causal = jnp.tril(jnp.ones((T, T), bool))
            wei = jnp.where(causal[None, None], wei, NEG_INF)
            wei = jnp.where(tgt_padding_mask[:, None, None, :], NEG_INF, wei)
            wei = jax.nn.softmax(wei, axis=-1)
            sa_out = _merge(jnp.einsum('bhts,bhsd->bhtd', wei, v)) @ sa_wproj + sa_bproj
            result = tgt + sa_out
            xq = _layernorm(result, ln2_g, ln2_b)
            xs = _layernorm(src, ln2_g, ln2_b)
            kv = xs @ ed_wkv
            k2, v2 = (_heads(t) for t in jnp.split(kv, 2, axis=-1))
            q2 = _heads(xq @ ed_wq)
            wei2 = jnp.einsum('bhtd,bhjd->bhtj', q2, k2) * scale
            wei2 = jax.nn.softmax(wei2, axis=-1)
            ed_out = _merge(jnp.einsum('bhtj,bhjd->bhtd', wei2, v2)) @ ed_wproj + ed_bproj
            result = result + ed_out
            h = jax.nn.relu(_layernorm(tgt, ln3_g, ln3_b) @ ff_w1 + ff_b1)
            result = result + (h @ ff_w2 + ff_b2)
            return result
        return _forward(tgt, src, sa_wqkv, sa_wproj, sa_bproj, ed_wkv, ed_wq, ed_wproj, ed_bproj, ff_w1, ff_b1, ff_w2, ff_b2, ln1_g, ln1_b, ln2_g, ln2_b, ln3_g, ln3_b, tgt_padding_mask)
    x = _L0_xattn_ref(x, ctx_1024, L0_xattn_sa_wqkv, L0_xattn_sa_wproj, L0_xattn_sa_bproj, L0_xattn_ed_wkv, L0_xattn_ed_wq, L0_xattn_ed_wproj, L0_xattn_ed_bproj, L0_xattn_ff_w1, L0_xattn_ff_b1, L0_xattn_ff_w2, L0_xattn_ff_b2, L0_xattn_ln1_g, L0_xattn_ln1_b, L0_xattn_ln2_g, L0_xattn_ln2_b, L0_xattn_ln3_g, L0_xattn_ln3_b, mask_BxS_bf0)
    return x

_drawn_inputs = setup_inputs


def setup_inputs(seed=0):
    import zlib

    import numpy as np

    out = dict(_drawn_inputs(seed))
    spreads = {'L0_xattn_sa_bproj': (0.0, 0.1),
     'L0_xattn_ed_bproj': (0.0, 0.1),
     'L0_xattn_ff_b1': (0.0, 0.1),
     'L0_xattn_ff_b2': (0.0, 0.1),
     'L0_xattn_ln1_g': (1.0, 0.6),
     'L0_xattn_ln1_b': (0.0, 0.426),
     'L0_xattn_ln2_g': (1.0, 0.6),
     'L0_xattn_ln2_b': (0.0, 0.401),
     'L0_xattn_ln3_g': (1.0, 0.2),
     'L0_xattn_ln3_b': (0.0, 0.281)}
    factors = {'L0_xattn_ed_wq': 8.0}
    for name, (base, spread) in spreads.items():
        noise = np.random.default_rng([zlib.crc32(name.encode()), seed]).standard_normal(out[name].shape)
        drawn = base * np.exp(spread * noise) if base else spread * noise
        out[name] = jnp.asarray(drawn.astype(out[name].dtype))
    for name, factor in factors.items():
        out[name] = (out[name] * factor).astype(out[name].dtype)
    return out
```

```python
from contextlib import ExitStack

import concourse.bass as bass
from concourse import mybir

ALU = mybir.AluOpType
ACT = mybir.ActivationFunctionType
AX_X = mybir.AxisListType.X
F32 = mybir.dt.float32
F32R = mybir.dt.float32r
U8 = mybir.dt.uint8

P = 128
LN_EPS = 1e-5
MASKED = -1e30

HI, LO = 0, 1
PASSES = ((HI, HI), (HI, LO), (LO, HI))


class Count:

    def __init__(self, sem, unit=1, primed=0):
        self.sem, self.unit, self.primed = sem, unit, primed

    def done(self, n):
        return (n + (1 + self.primed)) * self.unit

    def free(self, n):
        return (n + 1) * self.unit



class WeightSplitter:

    def __init__(self, units, stage, landed, hi_done, lo_done):
        self.units, self.stage, self.landed = units, stage, landed
        self.hi_done, self.lo_done = hi_done, lo_done

    def load(self, sp):
        depth = len(self.stage)
        for n, (src, _) in enumerate(self.units):
            if n >= depth:
                sp.wait_ge(self.lo_done, n - depth + 1)
            sp.dma_start(self.stage[n % depth], src).then_inc(self.landed[n % depth], 16)

    def round_hi(self, act, n):
        depth = len(self.stage)
        act.wait_ge(self.landed[n % depth], 16 * (n // depth + 1))
        act.copy(self.units[n][1][:, HI], self.stage[n % depth]).then_inc(self.hi_done, 1)

    def keep_lo(self, dve, n):
        dve.wait_ge(self.hi_done, n + 1)
        dve.tensor_tensor(self.units[n][1][:, LO], self.stage[n % len(self.stage)],
                          self.units[n][1][:, HI].bitcast(F32), ALU.subtract).then_inc(self.lo_done, 1)


class LayerNorm:

    def __init__(self, name, sem, sb, part, tiles, neg_half):
        self.part, self.tiles, self.neg_half = part, tiles, neg_half
        self.stats = sb(f"{name}_stats", [part, tiles + 1, 6], F32)
        self.mean_var = sb(f"{name}_mean_var", [part, tiles, 2], F32)
        self.var_eps = sb(f"{name}_var_eps", [part, tiles], F32)
        self.rstd = sb(f"{name}_rstd", [part, tiles], F32)
        self.stats_done = sem(f"{name}_stats_done")
        self.aggr_done = sem(f"{name}_aggr_done")
        self.eps_done = sem(f"{name}_eps_done")
        self.rstd_done = sem(f"{name}_rstd_done")
        self.xhat_done = sem(f"{name}_xhat_done")

    def statistics(self, dve, t, src):
        dve.bn_stats(self.stats[:, t, :], src).then_inc(self.stats_done, 1)

    def variance(self, dve, r):
        n = self.tiles
        dve.wait_ge(self.stats_done, r * n + n)
        dve.memset(self.stats[:, n, :], 0.0)
        for t in range(n):
            dve.bn_aggr(self.mean_var[:, t, :], self.stats[:, t, :]).then_inc(self.aggr_done, 1)
        dve.wait_ge(self.aggr_done, r * n + n)
        dve.tensor_scalar(self.var_eps[:], self.mean_var[:, :, 1], LN_EPS, None, ALU.add).then_inc(self.eps_done, 1)

    def inverse_root(self, pool, r):
        pool.wait_ge(self.eps_done, r + 1)
        pool.tensor_tensor(self.rstd[:], self.var_eps[:], self.neg_half[0:self.part, 0:self.tiles],
                           ALU.pow).then_inc(self.rstd_done, 1)

    def normalise(self, dve, r, t, src, dst):
        if t == 0:
            dve.wait_ge(self.rstd_done, r + 1)
        dve.tensor_scalar(dst, src, self.mean_var[:, t, 0:1], self.rstd[:, t:t + 1],
                          ALU.subtract, ALU.mult).then_inc(self.xhat_done, 1)


def product(pe, acc, lhs, rhs):
    steps = [(k, a, b) for k in range(4) for a, b in PASSES]
    for n, (k, a, b) in enumerate(steps):
        mm = pe.matmul(acc, lhs(a, k), rhs(b, k), start=n == 0, stop=n == len(steps) - 1)
    return mm


def feed_forward(nc, top, cn, x, ff_w1, ff_b1, ff_w2, ff_b2, ed_bproj, ln_params, ffn_out):
    B, T, C = x.shape
    FF = ff_w1.shape[1]
    KT, HT, CH = C // P, FF // P, FF // C
    TOK = 2 * P
    GROUPS = B * T // TOK
    x_rows = x.rearrange("b t c -> (b t) c").rearrange("(g t p) c -> g p t c", t=2, p=P)
    ffn_rows = ffn_out.rearrange("(g t p) c -> g p t c", t=2, p=P)

    with ExitStack() as ph:
        def sem(name):
            return top.enter_context(nc.semaphore("ff_" + name))

        def sb(name, shape, dt):
            return ph.enter_context(nc.sbuf_tensor("ff_" + name, shape, dt))

        def pb(name, shape):
            return ph.enter_context(nc.psum_tensor("ff_" + name, shape, F32))

        w1 = [sb(f"w1_{c}", [P, 2, KT, C], F32R) for c in range(CH)]
        w2 = [sb(f"w2_{c}", [P, 2, KT, C], F32R) for c in range(CH)]
        stage = [sb(f"stage{i}", [P, 2, C], F32)[:] for i in range(3)]
        xin = sb("xin", [P, 2, C], F32)
        xhat = sb("xhat", [P, 2, C], F32)
        xaff = sb("xaff", [P, KT, TOK], F32)
        xT = sb("xT", [P, 2, KT, TOK], F32R)
        hrelu = sb("hrelu", [P, 2, TOK], F32)
        hT = sb("hT", [P, 2, HT, TOK], F32R)
        y = sb("y", [P, 2, C], F32)
        bias = sb("bias", [P, 2, C], F32)
        vec_rows = sb("vec_rows", [6 * KT + HT, P], F32)
        b1 = cn["columns"][:, 6 * KT:]
        ps_x = pb("ps_x", [P, KT, TOK])
        ps_h = [pb(f"ps_h{i}", [P, 512]) for i in range(2)]
        ps_y = [pb(f"ps_y{i}", [P, 512]) for i in range(2)]

        x_landed, bias_landed = sem("x_landed"), sem("bias_landed")
        ln = LayerNorm("ff_ln", lambda n: top.enter_context(nc.semaphore(n)), sb, P, 2, cn["neg_half"])
        xT_psum, xaff_ready = sem("xT_psum"), sem("xaff_ready")
        xhi_ready, xlo_ready = sem("xhi_ready"), sem("xlo_ready")
        h_psum, y_psum = sem("h_psum"), sem("y_psum")
        relu_done = Count(sem("relu_done"), primed=2)
        hhi_done = sem("hhi_done")
        hlo_done = Count(sem("hlo_done"), primed=2)
        y_done = Count(sem("y_done"), primed=2)
        y_stored = [Count(sem(f"y_stored{t}"), unit=16, primed=1) for t in range(2)]
        bias_ready, vec_landed, vec_psum, columns_ready = (
            sem(n) for n in ("bias_ready", "vec_landed", "vec_psum", "columns_ready"))
        w1_v = ff_w1.rearrange("(k p) (c n) -> c p k n", p=P, n=C)
        w2_v = ff_w2.rearrange("(c k p) n -> c p k n", k=KT, p=P)
        units = [(v[c][:, 2 * h:2 * h + 2], w[c][:, :, 2 * h:2 * h + 2])
                 for v, w in ((w1_v, w1), (w2_v, w2)) for c in range(CH) for h in range(2)]
        ws = WeightSplitter(units, stage, [sem(f"w_landed{i}") for i in range(3)], sem("w_hi"), sem("w_lo"))

        with nc.Block() as block:
            @block.sync
            def _(sp):
                for t in range(2):
                    sp.sem_inc(y_stored[t].sem, 16)
                sp.dma_start(xin[:], x_rows[0]).then_inc(x_landed, 16)
                for n, v in enumerate(ln_params):
                    sp.dma_start(vec_rows[KT * n:KT * (n + 1), :], v.rearrange("(k p) -> k p", p=P)).then_inc(vec_landed, 16)
                sp.dma_start(vec_rows[6 * KT:, :], ff_b1.rearrange("(m p) -> m p", p=P)).then_inc(vec_landed, 16)
                sp.dma_start(bias[:, 0], ff_b2.partition_broadcast(P)).then_inc(bias_landed, 16)
                sp.dma_start(bias[:, 1], ed_bproj.partition_broadcast(P)).then_inc(bias_landed, 16)
                ws.load(sp)

                def group(g, last):
                    if not last:
                        sp.wait_ge(ln.xhat_done, 2 * g + 2)
                        sp.dma_start(xin[:], x_rows[g + 1]).then_inc(x_landed, 16)
                    for t in range(2):
                        sp.wait_ge(y_done.sem, y_done.done(2 * g + t))
                        sp.dma_start(ffn_rows[g][:, t], y[:, t]).then_inc(y_stored[t].sem, 16)

                with sp.Fori(0, GROUPS - 1) as g:
                    group(g, False)
                group(GROUPS - 1, True)
                for t in range(2):
                    sp.wait_ge(y_stored[t].sem, y_stored[t].done(GROUPS - 1))

            @block.gpsimd
            def _(pool):
                pool.sem_inc(hlo_done.sem, 2)
                ident, ready = cn["ident"], cn["ident_ready"]
                pool.memset(ident[:], 0.0).then_inc(ready, 1)
                pool.wait_ge(ready, 1)
                pool.affine_select(out=ident[:], in_=ident[:], compare_op=ALU.not_equal, fill=1.0, base=0,
                                   pattern=[[-1, P]], channel_multiplier=1).then_inc(ready, 1)
                pool.memset(cn["neg_half"][:], -0.5).then_inc(ready, 1)
                pool.wait_ge(ready, 3)

                def prepare(g):
                    ln.inverse_root(pool, g)
                    pool.wait_ge(xhi_ready, g + 1)
                    pool.tensor_tensor(xT[:, LO], xaff[:], xT[:, HI].bitcast(F32),
                                       ALU.subtract).then_inc(xlo_ready, 1)

                def group(g, last):
                    for m in range(HT):
                        pool.wait_ge(hhi_done, g * HT + m + 1)
                        pool.tensor_tensor(hT[:, LO, m], hrelu[:, m % 2], hT[:, HI, m].bitcast(F32),
                                           ALU.subtract).then_inc(hlo_done.sem, 1)
                    if not last:
                        prepare(g + 1)

                prepare(0)
                with pool.Fori(0, GROUPS - 1) as g:
                    group(g, False)
                group(GROUPS - 1, True)

            @block.scalar
            def _(act):
                act.sem_inc(relu_done.sem, 2)

                def prepare(g):
                    for k in range(KT):
                        act.wait_ge(xT_psum, g * KT + (k | 1) + 1)
                        act.activation(xaff[:, k], ps_x[:, k], ACT.Identity, bias=cn["columns"][:, 5 * KT + k:5 * KT + k + 1],
                                       scale=cn["columns"][:, 4 * KT + k:4 * KT + k + 1]).then_inc(xaff_ready, 1)

                def group(g, last, weights=False):
                    for m in range(HT):
                        if weights and m % KT == 0 and m < HT - KT:
                            for u in (0, 1):
                                ws.round_hi(act, m // 2 + 2 + u)
                        act.wait_ge(h_psum, g * HT + m + 1)
                        act.wait_ge(hlo_done.sem, hlo_done.free(g * HT + m))
                        act.activation(hrelu[:, m % 2], ps_h[m % 2][:, 0:TOK], ACT.Relu,
                                       bias=b1[:, m:m + 1]).then_inc(relu_done.sem, 1)
                    if weights:
                        for u in range(2 * CH, 4 * CH):
                            ws.round_hi(act, u)
                    if not last:
                        prepare(g + 1)

                act.wait_ge(vec_psum, 1)
                act.copy(cn["columns"][:], ps_h[0][:, 0:6 * KT + HT]).then_inc(columns_ready, 1)
                act.wait_ge(columns_ready, 1)
                for u in range(2):
                    ws.round_hi(act, u)
                prepare(0)
                group(0, False, weights=True)
                with act.Fori(1, GROUPS - 1) as g:
                    group(g, False)
                group(GROUPS - 1, True)

            @block.vector
            def _(dve):
                dve.sem_inc(y_done.sem, 2)

                def normalise(g):
                    dve.wait_ge(x_landed, 16 * g + 16)
                    for t in range(2):
                        ln.statistics(dve, t, xin[:, t])
                    ln.variance(dve, g)
                    for t in range(2):
                        ln.normalise(dve, g, t, xin[:, t], xhat[:, t])

                def tokens_hi(g):
                    dve.wait_ge(xaff_ready, KT * g + KT)
                    dve.tensor_copy(xT[:, HI], xaff[:]).then_inc(xhi_ready, 1)

                def result(g, t):
                    dve.wait_ge(y_psum, 2 * g + t + 1)
                    dve.wait_ge(y_stored[t].sem, y_stored[t].free(g))
                    dve.tensor_tensor(y[:, t], ps_y[t][:], bias[:, 0], ALU.add).then_inc(y_done.sem, 1)

                def group(g, last, weights=False):
                    for m in range(HT):
                        if weights and m % KT == 0 and m < HT - KT:
                            for u in (0, 1):
                                ws.keep_lo(dve, m // 2 + 2 + u)
                        dve.wait_ge(relu_done.sem, relu_done.done(g * HT + m))
                        dve.tensor_copy(hT[:, HI, m], hrelu[:, m % 2]).then_inc(hhi_done, 1)
                    if weights:
                        for u in range(2 * CH, 4 * CH):
                            ws.keep_lo(dve, u)
                    if not last:
                        normalise(g + 1)
                    result(g, 0)
                    if not last:
                        tokens_hi(g + 1)
                    result(g, 1)

                normalise(0)
                for u in range(2):
                    ws.keep_lo(dve, u)
                dve.wait_ge(bias_landed, 32)
                dve.tensor_tensor(bias[:, 0], bias[:, 0], bias[:, 1], ALU.add).then_inc(bias_ready, 1)
                tokens_hi(0)
                dve.wait_ge(bias_ready, 1)
                group(0, False, weights=True)
                with dve.Fori(1, GROUPS - 1) as g:
                    group(g, False)
                group(GROUPS - 1, True)

            @block.tensor
            def _(pe):
                def transposes(g):
                    for k in range(KT):
                        for t in range(2):
                            if k == 0:
                                pe.wait_ge(ln.xhat_done, 2 * g + t + 1)
                            mm = pe.transpose(ps_x[:, k, P * t:P * (t + 1)], xhat[:, t, P * k:P * (k + 1)],
                                              cn["ident"][:])
                        mm.then_inc(xT_psum, 1)

                def hidden(g, weights=False):
                    pe.wait_ge(xlo_ready, g + 1)
                    for m in range(HT):
                        c, n = m // KT, m % KT
                        if weights and n == 0:
                            pe.wait_ge(ws.lo_done, 2 * c + 2)
                        pe.wait_ge(relu_done.sem, relu_done.free(g * HT + m))
                        product(pe, ps_h[m % 2][:, 0:TOK], lambda a, k: w1[c][:, a, k, P * n:P * (n + 1)],
                                lambda b, k: xT[:, b, k, :]).then_inc(h_psum, 1)

                def result(g, t, weights=False):
                    pe.wait_ge(y_done.sem, y_done.free(2 * g + t))
                    for c in range(CH):
                        if weights:
                            pe.wait_ge(ws.lo_done, 2 * CH + 2 * c + 2)
                        for k in range(KT):
                            m = c * KT + k
                            for a, b in PASSES:
                                mm = pe.matmul(ps_y[t][:], hT[:, a, m, P * t:P * (t + 1)], w2[c][:, b, k, :],
                                               start=(m == 0 and (a, b) == PASSES[0]),
                                               stop=(m == HT - 1 and (a, b) == PASSES[-1]))
                    mm.then_inc(y_psum, 1)

                def group(g, last, weights=False):
                    hidden(g, weights)
                    pe.wait_ge(hlo_done.sem, hlo_done.done(g * HT + HT - 1))
                    result(g, 0, weights)
                    if not last:
                        transposes(g + 1)
                    result(g, 1)

                pe.wait_ge(cn["ident_ready"], 3)
                pe.wait_ge(vec_landed, 16 * 7)
                pe.transpose(ps_h[0][:, 0:6 * KT + HT], vec_rows[:], cn["ident"][0:6 * KT + HT, 0:6 * KT + HT])\
                    .then_inc(vec_psum, 1)
                pe.wait_ge(columns_ready, 1)
                transposes(0)
                group(0, False, weights=True)
                with pe.Fori(1, GROUPS - 1) as g:
                    group(g, False)
                group(GROUPS - 1, True)


def xattn_kernel(nc, x, ctx_in, mask, wqkv, wproj, bproj, ed_wkv, ed_wq, ed_wproj, ed_bproj,
                 ff_w1, ff_b1, ff_w2, ff_b2, ln1_g, ln1_b, ln2_g, ln2_b, ln3_g, ln3_b, out):
    B, T, C = x.shape
    FF = ff_w1.shape[1]
    KT = C // P
    ffn_out = nc.dram_tensor("ffn_out", (B * T, C), F32, kind="Internal").ap()
    res_out = nc.dram_tensor("res_out", (B, T, C), F32, kind="Internal").ap()
    qk_rows = nc.dram_tensor("qk_rows", (B, 2, 2, C, T), F32, kind="Internal").ap()
    q2_out = nc.dram_tensor("q2_out", (B, 2, KT, P, T), F32, kind="Internal").ap()
    with ExitStack() as top:
        cn = {
            "ident": top.enter_context(nc.sbuf_tensor("ident", [P, P], F32)),
            "columns": top.enter_context(nc.sbuf_tensor("columns", [P, 6 * KT + FF // P], F32)),
            "neg_half": top.enter_context(nc.sbuf_tensor("neg_half", [P, 8], F32)),
            "ident_ready": top.enter_context(nc.semaphore("ident_ready")),
        }
        feed_forward(nc, top, cn, x, ff_w1, ff_b1, ff_w2, ff_b2, ed_bproj,
                     (ln1_g, ln1_b, ln2_g, ln2_b, ln3_g, ln3_b), ffn_out)
        self_attention(nc, top, cn, x, mask, wqkv, wproj, bproj, ed_wq, ffn_out, qk_rows, res_out, q2_out)
        cross_attention(nc, top, cn, ctx_in, ed_wkv, ed_wproj, res_out, q2_out, out)


def plan_self_attention(kind):
    ahead = [("T", 0), ("T", 1)] + [("Q", m) for m in range(4)] + [("K", m) for m in range(4)] + [("V", 0), ("V", 1)]
    if kind == "first":
        return ahead
    fill = {3: ("T", 0), 4: ("T", 1), 6: ("Q", 0), 7: ("Q", 1), 9: ("Q", 2), 10: ("Q", 3), 12: ("K", 0), 14: ("K", 1)}
    items = []
    for i in range(16 + 3):
        if i < 16:
            items.append(("head", i))
        if i >= 3:
            items.append(("prob", i - 3))
        if i >= 7 and i % 4 == 3 and i < 18:
            items.append(("value", (i - 7) // 4))
        if i in fill and kind != "last":
            items.append(fill[i])
    tail = [("K", 2), ("value", 3), ("K", 3), ("P", 0), ("P", 1), ("V", 0), ("V", 1), ("R", 0), ("R", 1)]
    tail += [("Y", m) for m in range(4)]
    return items + [t for t in tail if kind != "last" or t[0] not in "KV"]


def numbered(plan):
    acc = f32 = split = 0
    out = []
    for name, m in plan:
        out.append((name, m, acc, f32, split))
        if name in ("T", "Q", "K", "V", "P", "R", "Y"):
            acc += 1
            f32 += name != "V"
            split += name not in ("V", "P")
    return out


def self_attention(nc, top, cn, x, mask, wqkv, wproj, bproj, ed_wq, ffn_out, qk_rows, res_out, q2_out):
    B, T, C = x.shape
    KT = C // P
    H, HD, GH = 16, 32, 4
    TQ = T // 2
    SCALE = float(C) ** -0.5
    STACK_Q, STACK_K = (HI, LO, HI), (HI, HI, LO)
    KS = 3 * HD
    STACKED = 16 * 2 * 3
    ACC0, F0, SP0 = 12, 10, 10
    ACCN, FN, SPN = 20, 18, 16

    with ExitStack() as ph:
        def sem(name):
            return top.enter_context(nc.semaphore("sa_" + name))

        def sb(name, shape, dt):
            return ph.enter_context(nc.sbuf_tensor("sa_" + name, shape, dt))

        def pb(name, shape):
            return ph.enter_context(nc.psum_tensor("sa_" + name, shape, F32))

        w = {n: sb(f"w_{n}", [P, 2, KT, C], F32R) for n in "qkvpy"}
        xin = sb("xin", [TQ, 2, C], F32)
        xhat = sb("xhat", [TQ, 2, C], F32)
        res = sb("res", [TQ, 2, C], F32)
        fin = sb("fin", [TQ, 2, C], F32)
        bias = sb("bias", [TQ, C], F32)
        xT = sb("xT", [P, 2, KT, T], F32R)
        rT = sb("rT", [P, 2, KT, T], F32R)
        f32 = sb("f32", [P, 2, C], F32)
        qT = sb("qT", [P, 2, KT, T], F32R)
        kT = sb("kT", [P, 2, KT, T], F32R)
        q_stack = sb("q_stack", [KS, H, T], F32R)
        k_stack = sb("k_stack", [KS, H, T], F32R)
        v = sb("v", [TQ, 2, C], F32)
        prob = sb("prob", [TQ, 4, 2, T], F32)
        probT = sb("probT", [P, 8, T + TQ], F32)
        maxes = sb("maxes", [TQ, 4, 2], F32)
        sums = sb("sums", [TQ, 2, 2, GH], F32)
        inv = sb("inv", [TQ, 2, GH], F32)
        rinv = sb("rinv", [TQ, 2, 2, P], F32)
        rinv_T = sb("rinv_T", [P, 2, T], F32)
        of = sb("of", [P, 2, T], F32)
        oT = sb("oT", [P, 2, KT, T], F32R)
        yT = sb("yT", [P, 2, KT, T], F32R)
        mask_u8 = sb("mask_u8", [TQ, T], U8)
        mask_f = sb("mask_f", [TQ, T], F32)
        causal = sb("causal", [TQ, 2, T], F32)
        masks = sb("masks", [TQ, 2, T], F32)
        stage_t = probT[:].rearrange("p a b -> p (a b)")
        stage = [stage_t[:, 2 * C * i:2 * C * (i + 1)].rearrange("p (k n) -> p k n", k=2) for i in range(2)]
        ps_s = [pb(f"ps_s{i}", [P, 512]) for i in range(2)]
        ps_t = [pb(f"ps_t{i}", [P, 512]) for i in range(2)]
        ps_o = [pb(f"ps_o{i}", [P, 512]) for i in range(2)]
        ps_acc = [pb(f"ps_acc{i}", [P, 512]) for i in range(2)]

        mk_sem = lambda n: top.enter_context(nc.semaphore(n))
        ln1 = LayerNorm("sa_ln1", mk_sem, sb, TQ, 2, cn["neg_half"])
        ln2 = LayerNorm("sa_ln2", mk_sem, sb, TQ, 2, cn["neg_half"])
        x_landed, mask_landed, res_landed, fin_landed, bias_landed = (
            sem(n) for n in ("x_landed", "mask_landed", "res_landed", "fin_landed", "bias_landed"))
        rows_written = [sem(f"rows_written{m}") for m in range(KT)]
        stacked = [sem(f"stacked{i}") for i in range(2)]
        causal_ready, mask_ready, masks_ready, bias_added = (
            sem(n) for n in ("causal_ready", "mask_ready", "masks_ready", "bias_added"))
        s_psum, max_done, exp_done, inv_done, recip_done = (
            sem(n) for n in ("s_psum", "max_done", "exp_done", "inv_done", "recip_done"))
        s_masked = Count(sem("s_masked"), primed=2)
        t_psum, o_psum, rinvT_done, ohi_done = (sem(n) for n in ("t_psum", "o_psum", "rinvT_done", "ohi_done"))
        probT_done = Count(sem("probT_done"), primed=2)
        of_done = Count(sem("of_done"), primed=2)
        olo_done = Count(sem("olo_done"), primed=2)
        acc_psum = sem("acc_psum")
        acc_read = Count(sem("acc_read"), primed=2)
        hi_done = sem("hi_done")
        f_free = Count(sem("f_free"), primed=2)
        fin_done = Count(sem("fin_done"), primed=2)
        res_stored = Count(sem("res_stored"), unit=16, primed=1)
        y_stored = Count(sem("y_stored"), unit=32, primed=1)

        w_views = {"q": wqkv[:, 0:C], "k": wqkv[:, C:2 * C], "v": wqkv[:, 2 * C:3 * C], "p": wproj, "y": ed_wq}
        units = [(w_views[n].rearrange("(k p) n -> p k n", p=P)[:, 2 * h:2 * h + 2], w[n][:, :, 2 * h:2 * h + 2])
                 for n in "qkvpy" for h in range(2)]
        ws = WeightSplitter(units, stage, [sem(f"w_landed{i}") for i in range(2)], sem("w_hi"), sem("w_lo"))
        weights_before = {("T", 0): range(0, 2), ("K", 0): range(2, 4), ("V", 0): range(4, 6)}
        plans = {k: numbered(plan_self_attention(k)) for k in ("first", "body", "last")}

        def f_tile(name, f):
            if name in ("T", "R"):
                return f32[:, f % 2, 0:2 * T].rearrange("p (k t) -> p k t", k=2)
            if name == "P":
                return f32[0:TQ, f % 2, :]
            return f32[:, f % 2, 0:T]

        def split_dst(name, m, half):
            if name in ("T", "R"):
                return (xT if name == "T" else rT)[:, half, 2 * m:2 * m + 2, :]
            return {"Q": qT, "K": kT, "Y": yT}[name][:, half, m, :]

        def run(eng, step, after=None):
            step("first", -1, plans["first"])
            if after is not None:
                after()
            with eng.Fori(0, B - 1) as b:
                step("body", b, plans["body"])
            step("last", B - 1, plans["last"])

        def bases(kind, b):
            return (0, 0, 0) if kind == "first" else (ACC0 + ACCN * b, F0 + FN * b, SP0 + SPN * b)

        with nc.Block() as block:
            @block.sync
            def _(sp):
                sp.sem_inc(res_stored.sem, 16)
                sp.sem_inc(y_stored.sem, 32)
                tokens = lambda a, b: a[b].rearrange("(t p) c -> p t c", p=TQ)
                ffn_tokens = ffn_out.rearrange("(b t) c -> b t c", b=B)
                mask_row = lambda b: mask[b].partition_broadcast(TQ)
                sp.dma_start(xin[:], tokens(x, 0)).then_inc(x_landed, 16)
                sp.dma_start(mask_u8[:], mask_row(0)).then_inc(mask_landed, 16)
                sp.dma_start(bias[:], bproj.partition_broadcast(TQ)).then_inc(bias_landed, 16)
                ws.load(sp)

                def write_rows(name, m, n, b, f0):
                    sp.wait_ge(f_free.sem, f_free.done(f0 + n))
                    src, dst = (qT, qk_rows[b + 1, 0]) if name == "Q" else (kT, qk_rows[b + 1, 1])
                    sp.dma_start(dst[:, P * m:P * (m + 1)].rearrange("a p t -> p a t"), src[:, :, m, :].bitcast(F32))\
                        .then_inc(rows_written[m], 16)

                def stack(kind, pair, b):
                    if kind == "body":
                        sp.wait_ge(s_psum, 16 * b + (8 * pair + 8))
                    for m in (2 * pair, 2 * pair + 1):
                        sp.wait_ge(rows_written[m], 32 * b + 64)
                    heads = slice(8 * pair, 8 * pair + 8)
                    for i, (dst, order) in enumerate(((q_stack, STACK_Q), (k_stack, STACK_K))):
                        for c, half in enumerate(order):
                            sp.dma_start(
                                dst[HD * c:HD * (c + 1), heads, :].bitcast(F32),
                                qk_rows[b + 1, i, half, 2 * P * pair:2 * P * (pair + 1)].rearrange(
                                    "(h d) t -> d h t", d=HD)).then_inc(stacked[pair], 16)

                def step(kind, b, items, next_x=True):
                    _, f0, _ = bases(kind, b)
                    if kind == "first":
                        sp.wait_ge(ln1.xhat_done, 2)
                        sp.dma_start(xin[:], tokens(x, 1)).then_inc(x_landed, 16)
                        sp.wait_ge(mask_ready, 1)
                        sp.dma_start(mask_u8[:], mask_row(1)).then_inc(mask_landed, 16)
                    else:
                        sp.wait_ge(fin_done.sem, fin_done.free(2 * b + 1))
                        sp.dma_start(res[:], tokens(x, b)).then_inc(res_landed, 16)
                        sp.wait_ge(res_stored.sem, res_stored.free(b))
                        sp.dma_start(fin[:], tokens(ffn_tokens, b)).then_inc(fin_landed, 16)
                        if next_x:
                            sp.wait_ge(ln1.xhat_done, 2 * b + 4)
                            sp.dma_start(xin[:], tokens(x, b + 2)).then_inc(x_landed, 16)
                    for name, m, acc, f, _ in items:
                        if name in ("Q", "K"):
                            write_rows(name, m, f, b, f0)
                            if name == "K" and m % 2 == 1:
                                stack(kind, m // 2, b)
                        if name == "Y" and m == 0:
                            sp.wait_ge(fin_done.sem, fin_done.done(2 * b + 1))
                            sp.dma_start(tokens(res_out, b), fin[:]).then_inc(res_stored.sem, 16)
                            if next_x:
                                sp.dma_start(mask_u8[:], mask_row(b + 2)).then_inc(mask_landed, 16)
                        if name == "Y" and m == KT - 1:
                            sp.wait_ge(f_free.sem, f_free.done(f0 + f))
                            for half in (HI, LO):
                                sp.dma_start(q2_out[b, half].rearrange("k p t -> p k t"),
                                             yT[:, half].bitcast(F32)).then_inc(y_stored.sem, 16)

                step("first", -1, plans["first"])
                with sp.Fori(0, B - 2) as b:
                    step("body", b, plans["body"])
                step("body", B - 2, plans["body"], next_x=False)
                step("last", B - 1, plans["last"], next_x=False)
                sp.wait_ge(res_stored.sem, res_stored.done(B - 1))
                sp.wait_ge(y_stored.sem, y_stored.done(B - 1))

            @block.gpsimd
            def _(pool):
                pool.sem_inc(f_free.sem, 2)
                pool.sem_inc(olo_done.sem, 2)
                pool.sem_inc(fin_done.sem, 2)
                pool.memset(causal[:], 0.0).then_inc(causal_ready, 1)
                pool.wait_ge(causal_ready, 1)
                pool.affine_select(out=causal[:], in_=causal[:], compare_op=ALU.is_ge, fill=MASKED, base=0,
                                   pattern=[[TQ, 2], [-1, T]], channel_multiplier=1).then_inc(causal_ready, 1)

                def step(kind, b, items):
                    acc0, f0, sp0 = bases(kind, b)
                    if kind != "last":
                        ln1.inverse_root(pool, b + 1)
                    for name, m, acc, f, s in items:
                        if name in ("T", "Q", "K", "R", "Y"):
                            pool.wait_ge(hi_done, sp0 + (s + 1))
                            pool.tensor_tensor(split_dst(name, m, LO), f_tile(name, f),
                                               split_dst(name, m, HI).bitcast(F32), ALU.subtract)\
                                .then_inc(f_free.sem, 1)
                        if name == "value":
                            pool.wait_ge(ohi_done, KT * b + (m + 1))
                            pool.tensor_tensor(oT[:, LO, m], of[:, m % 2], oT[:, HI, m].bitcast(F32),
                                               ALU.subtract).then_inc(olo_done.sem, 1)
                        if name == "P":
                            if m == 0:
                                pool.wait_ge(bias_added, 2 * b + 2)
                            pool.wait_ge(acc_read.sem, acc_read.done(acc0 + acc))
                            pool.tensor_tensor(res[:, m], f_tile(name, f), res[:, m], ALU.add)\
                                .then_inc(f_free.sem, 1)
                            if m == 1:
                                ln2.inverse_root(pool, b)
                                pool.wait_ge(fin_landed, 16 * b + 16)
                                for t in range(2):
                                    pool.tensor_tensor(fin[:, t], res[:, t], fin[:, t], ALU.add)\
                                        .then_inc(fin_done.sem, 1)

                run(pool, step)

            @block.scalar
            def _(act):
                act.sem_inc(acc_read.sem, 2)

                def step(kind, b, items):
                    acc0, f0, _ = bases(kind, b)
                    for name, m, acc, f, _ in items:
                        if kind == "first":
                            for u in weights_before.get((name, m), ()):
                                ws.round_hi(act, u)
                        if name == "head":
                            act.wait_ge(max_done, 16 * b + (m + 1))
                            for q in range(2):
                                ins = act.activation(prob[:, m % 4, q], prob[:, m % 4, q], ACT.Exp,
                                                     bias=maxes[:, m % 4, q:q + 1], accum_out=sums[:, (m // GH) % 2, q, m % GH:m % GH + 1])
                            ins.then_inc(exp_done, 1)
                        if name == "value":
                            act.wait_ge(o_psum, KT * b + (m + 1))
                            act.copy(rinv_T[:, m % 2], ps_o[m % 2][:, T:2 * T]).then_inc(rinvT_done, 1)
                        if name not in ("T", "Q", "K", "V", "P", "R", "Y"):
                            continue
                        a = ps_acc[acc % 2]
                        act.wait_ge(acc_psum, acc0 + (acc + 1))
                        if name != "V":
                            act.wait_ge(f_free.sem, f_free.free(f0 + f))
                        if name in ("T", "R"):
                            gain = (0 if name == "T" else 2) * KT + 2 * m
                            for k in range(2):
                                ins = act.activation(f_tile(name, f)[:, k], a[:, T * k:T * (k + 1)], ACT.Identity,
                                                     bias=cn["columns"][:, gain + KT + k:gain + KT + k + 1],
                                                     scale=cn["columns"][:, gain + k:gain + k + 1])
                        elif name in ("Q", "Y"):
                            ins = act.mul(f_tile(name, f), a[:, 0:T], SCALE)
                        elif name == "K":
                            ins = act.copy(f_tile(name, f), a[:, 0:T])
                        else:
                            ins = act.copy(f_tile(name, f) if name == "P" else v[:, m], a[0:TQ, :])
                        ins.then_inc(acc_read.sem, 1)

                run(act, step, lambda: [ws.round_hi(act, u) for u in range(6, 10)])

            @block.vector
            def _(dve):
                dve.sem_inc(s_masked.sem, 2)
                dve.sem_inc(probT_done.sem, 2)
                dve.sem_inc(of_done.sem, 2)

                def build_masks(b):
                    dve.wait_ge(mask_landed, 16 * b + 16)
                    dve.tensor_scalar(mask_f[:], mask_u8[:], MASKED, None, ALU.mult).then_inc(mask_ready, 1)
                    dve.wait_ge(mask_ready, b + 1)
                    for q in range(2):
                        ins = dve.tensor_tensor(masks[:, q], causal[:, q], mask_f[:], ALU.add)
                    ins.then_inc(masks_ready, 1)

                def token_statistics(b):
                    dve.wait_ge(x_landed, 16 * b + 16)
                    for t in range(2):
                        ln1.statistics(dve, t, xin[:, t])
                    ln1.variance(dve, b)

                def normalise_tokens(b):
                    for t in range(2):
                        ln1.normalise(dve, b, t, xin[:, t], xhat[:, t])

                def split_hi(kind, b, item):
                    acc0, _, _ = bases(kind, b)
                    name, m, acc, f, s = item
                    dve.wait_ge(acc_read.sem, acc_read.done(acc0 + acc))
                    if kind == "body" and name in ("Q", "K"):
                        dve.wait_ge(rows_written[m], 32 * b + 32)
                    if name == "Y" and m == 0:
                        dve.wait_ge(y_stored.sem, y_stored.free(b))
                    dve.tensor_copy(split_dst(name, m, HI), f_tile(name, f)).then_inc(hi_done, 1)

                def step(kind, b, items):
                    if kind == "first":
                        token_statistics(0)
                        normalise_tokens(0)
                    held = None
                    for item in items:
                        name, m = item[:2]
                        if kind == "first":
                            for u in weights_before.get((name, m), ()):
                                ws.keep_lo(dve, u)
                        if name == "head":
                            dve.wait_ge(s_psum, 16 * b + (m + 1))
                            if m == 0:
                                dve.wait_ge(masks_ready, b + 1)
                            dve.tensor_tensor(prob[:, m % 4], ps_s[m % 2][0:TQ, 0:2 * T].rearrange(
                                "p (q t) -> p q t", q=2), masks[:], ALU.add).then_inc(s_masked.sem, 1)
                            dve.wait_ge(s_masked.sem, s_masked.done(16 * b + m))
                            dve.tensor_reduce(maxes[:, m % 4], prob[:, m % 4], AX_X, ALU.max, negate=True)\
                                .then_inc(max_done, 1)
                            if held is not None:
                                split_hi(kind, b, held)
                                held = None
                            if m == 0 and kind == "body":
                                token_statistics(b + 1)
                            if m == 1 and kind == "body":
                                normalise_tokens(b + 1)
                            if m == 2:
                                dve.wait_ge(res_landed, 16 * b + 16)
                                for t in range(2):
                                    dve.tensor_tensor(res[:, t], res[:, t], bias[:], ALU.add).then_inc(bias_added, 1)
                        if (name == "head" and m % GH == 0 and m) or (name == "prob" and m == 13):
                            g = m // GH - 1 if name == "head" else KT - 1
                            dve.wait_ge(exp_done, 16 * b + (GH * g + GH))
                            dve.reciprocal(inv[:], sums[:, g % 2]).then_inc(inv_done, 1)
                            dve.wait_ge(inv_done, KT * b + (g + 1))
                            dve.tensor_copy(rinv[:, g % 2].rearrange("p q (j d) -> p q j d", d=HD),
                                            inv[:].unsqueeze(3).to_broadcast([TQ, 2, GH, HD])).then_inc(recip_done, 1)
                        if name == "prob":
                            dve.wait_ge(t_psum, 16 * b + (m + 1))
                            dve.tensor_copy(probT[0:TQ, m % 8], ps_t[m % 2][0:TQ, 0:T + TQ])\
                                .then_inc(probT_done.sem, 1)
                        if name == "value":
                            dve.wait_ge(rinvT_done, KT * b + (m + 1))
                            dve.wait_ge(olo_done.sem, olo_done.free(KT * b + m))
                            dve.tensor_tensor(of[:, m % 2], ps_o[m % 2][:, 0:T], rinv_T[:, m % 2], ALU.mult)\
                                .then_inc(of_done.sem, 1)
                            dve.wait_ge(of_done.sem, of_done.done(KT * b + m))
                            dve.tensor_copy(oT[:, HI, m], of[:, m % 2]).then_inc(ohi_done, 1)
                        if name in ("T", "Q", "K", "R", "Y"):
                            if kind == "body" and item[2] < 8:
                                assert held is None
                                held = item
                            else:
                                if held is not None:
                                    split_hi(kind, b, held)
                                    held = None
                                split_hi(kind, b, item)
                        if name == "prob" and m == 15:
                            if held is not None:
                                split_hi(kind, b, held)
                                held = None
                            if kind == "body":
                                build_masks(b + 1)
                        if name == "P" and m == 1:
                            for t in range(2):
                                dve.wait_ge(f_free.sem, f_free.done(bases(kind, b)[1] + item[3] - 1 + t))
                                ln2.statistics(dve, t, res[:, t])
                            ln2.variance(dve, b)
                            for t in range(2):
                                ln2.normalise(dve, b, t, res[:, t], xhat[:, t])

                def after_first():
                    for u in range(6, 10):
                        ws.keep_lo(dve, u)
                    dve.wait_ge(causal_ready, 2)
                    build_masks(0)
                    dve.wait_ge(bias_landed, 16)

                run(dve, step, after_first)

            @block.tensor
            def _(pe):
                def step(kind, b, items):
                    acc0, f0, _ = bases(kind, b)
                    ready = {(i[0], i[1]): f0 + i[3] for i in items}
                    for name, m, acc, f, _ in items:
                        if kind == "first" and (name, m) in weights_before:
                            pe.wait_ge(ws.lo_done, weights_before[name, m][-1] + 1)
                        if name == "head":
                            if m % 8 == 0:
                                pe.wait_ge(stacked[m // 8], STACKED * b + STACKED)
                            pe.wait_ge(s_masked.sem, s_masked.free(16 * b + m))
                            for q in range(2):
                                mm = pe.matmul(ps_s[m % 2][0:TQ, T * q:T * (q + 1)],
                                               q_stack[:, m, TQ * q:TQ * (q + 1)], k_stack[:, m, :],
                                               start=True, stop=True)
                            mm.then_inc(s_psum, 1)
                        if name == "prob":
                            pe.wait_ge(exp_done, 16 * b + (m + 1))
                            pe.wait_ge(probT_done.sem, probT_done.free(16 * b + m))
                            t, id_q = ps_t[m % 2], cn["ident"][0:TQ, 0:TQ]
                            pe.transpose(t[0:TQ, 0:TQ], prob[:, m % 4, 0, 0:TQ], id_q)
                            pe.transpose(t[0:TQ, TQ:T], prob[:, m % 4, 1, 0:TQ], id_q)
                            pe.transpose(t[0:TQ, T:T + TQ], prob[:, m % 4, 1, TQ:T], id_q).then_inc(t_psum, 1)
                        if name == "value":
                            o = ps_o[m % 2]
                            pe.wait_ge(of_done.sem, of_done.free(KT * b + m))
                            pe.wait_ge(recip_done, KT * b + (m + 1))
                            for q in range(2):
                                pe.transpose(o[:, T + TQ * q:T + TQ * (q + 1)],
                                             rinv[:, m % 2, q, :],
                                             cn["ident"][0:TQ, 0:TQ])
                            pe.wait_ge(probT_done.sem, probT_done.done(16 * b + (GH * m + GH - 1)))
                            for kt, cols in ((0, slice(0, T)), (1, slice(TQ, T))):
                                for j in range(GH):
                                    h = GH * m + j
                                    src = probT[0:TQ, h % 8, 0:T] if kt == 0 else probT[0:TQ, h % 8, T:T + TQ]
                                    mm = pe.matmul(o[HD * j:HD * (j + 1), cols], v[:, kt, HD * h:HD * (h + 1)], src,
                                                   start=kt == 0, stop=kt == 1)
                            mm.then_inc(o_psum, 1)
                        if name not in ("T", "Q", "K", "V", "P", "R", "Y"):
                            continue
                        a = ps_acc[acc % 2]
                        pe.wait_ge(acc_read.sem, acc_read.free(acc0 + acc))
                        if name in ("T", "R"):
                            ln = ln1 if name == "T" else ln2
                            if m == 0:
                                pe.wait_ge(ln.xhat_done, 2 * b + (4 if name == "T" else 2))
                            for k in range(2):
                                for t in range(2):
                                    mm = pe.transpose(a[:, T * k + TQ * t:T * k + TQ * (t + 1)],
                                                      xhat[:, t, P * (2 * m + k):P * (2 * m + k + 1)],
                                                      cn["ident"][0:TQ, 0:TQ])
                        elif name in ("Q", "K", "Y"):
                            src, wt = (rT, w["y"]) if name == "Y" else (xT, w[name.lower()])
                            if m == 0 and name != "K":
                                pe.wait_ge(f_free.sem, f_free.done(ready["R" if name == "Y" else "T", 1]))
                            mm = product(pe, a[:, 0:T], lambda c, k: wt[:, c, k, P * m:P * (m + 1)],
                                         lambda c, k: src[:, c, k, :])
                        else:
                            src, wt = (xT, w["v"]) if name == "V" else (oT, w["p"])
                            if name == "P" and m == 0:
                                pe.wait_ge(olo_done.sem, olo_done.done(KT * b + KT - 1))
                            mm = product(pe, a[0:TQ, :], lambda c, k: src[:, c, k, TQ * m:TQ * (m + 1)],
                                         lambda c, k: wt[:, c, k, :])
                        mm.then_inc(acc_psum, 1)

                run(pe, step, lambda: pe.wait_ge(ws.lo_done, 10))


def plan_cross_attention(kind):
    ahead = [("T", k, a) for k in range(4) for a in range(2)]
    keys = [[("K", m, a) for a in range(2)] for m in range(4)]
    if kind == "first":
        return [i for t in ahead + keys[0] + keys[1] + keys[2] for i in (t, ("hi", t))]
    fill = {i: [("V", i, 0)] for i in range(6)}
    fill.update({6: keys[3][:1], 7: keys[3][1:]})
    if kind == "body":
        fill.update({10 + i: [ahead[i]] for i in range(8)})
        fill.update({20: keys[0][:1], 21: keys[0][1:], 25: keys[1][:1], 26: keys[1][1:],
                     32: keys[2][:1], 33: keys[2][1:]})
    items, late = [], []
    for i in range(36):
        if 3 <= i < 35:
            items.append(("probT", i - 3))
        if i < 32:
            items.append(("score", i))
        items += late
        late = []
        if i >= 7 and i % 4 == 3:
            if i == 35:
                items.append(("E", 0, 0))
            items.append(("value", (i - 7) // 4))
            late.append(("scale", (i - 7) // 4))
        for t in fill.get(i, ()):
            items.append(t)
            if t[0] in "KT":
                late.append(("hi", t))
    return items + late + [("E", 1, 0)]


def numbered_uses(plan):
    acc = f32 = split = 0
    out, seen = [], {}
    for item in plan:
        if item[0] == "hi":
            out.append(("hi", item[1]) + seen[item[1]])
            continue
        seen[item] = (acc, f32, split)
        out.append((item[0], item[1:]) + seen[item])
        if item[0] in ("V", "K", "T", "E"):
            acc += 1
            f32 += item[0] != "V"
            split += item[0] in ("K", "T")
    return out


def cross_attention(nc, top, cn, ctx_in, ed_wkv, ed_wproj, res_out, q2_out, out):
    B, T, C = out.shape
    J = ctx_in.shape[1]
    KT = C // P
    H, HD, GH = 16, 32, 4
    TQ = T // 2
    NT = 6
    JT = J // NT
    JH = J // 2
    JP = JH + 1
    STACK_Q, STACK_K = (HI, LO, HI), (HI, HI, LO)
    KS = 3 * HD
    STACKED_K, STACKED_Q = 16 * 3 * GH, 16 * 3
    ACC0, ACCN, FN, SPN = 14, 24, 18, 16
    SC, UN = 32, 8

    with ExitStack() as ph:
        def sem(name):
            return top.enter_context(nc.semaphore("ca_" + name))

        def sb(name, shape, dt):
            return ph.enter_context(nc.sbuf_tensor("ca_" + name, shape, dt))

        def pb(name, shape):
            return ph.enter_context(nc.psum_tensor("ca_" + name, shape, F32))

        wk = sb("wk", [P, 2, KT, C], F32R)
        wv = sb("wv", [P, 2, KT, C], F32R)
        wp = sb("wp", [P, KT, C], F32)
        xs = sb("xs", [JT, NT, C], F32)
        xT = sb("xT", [P, 2, KT, 2, JP], F32R)
        f32 = sb("f32", [P, 2, C], F32)
        keys = sb("keys", [P, 2, 2, JP], F32R)
        k_stack = sb("k_stack", [KS, H, 2, JP], F32R)
        q_stack = sb("q_stack", [KS, H, T], F32R)
        v = sb("v", [JT, NT, C], F32)
        prob = sb("prob", [TQ, 4, 2, JH], F32)
        probT = sb("probT", [P, 2, GH, NT, TQ], F32)
        maxes = sb("maxes", [TQ, 4], F32)
        sums = sb("sums", [TQ, 2, GH], F32)
        inv = sb("inv", [TQ, GH], F32)
        rinv = sb("rinv", [TQ, P], F32)
        rinv_T = sb("rinv_T", [P, TQ], F32)
        oT = sb("oT", [P, KT, T], F32)
        res = sb("res", [TQ, 2, C], F32)
        stage_t = probT[:].rearrange("p a b c d -> p (a b c d)")
        stage = [stage_t[:, 2 * C * i:2 * C * (i + 1)].rearrange("p (k n) -> p k n", k=2) for i in range(2)]
        ps_s = [pb(f"ps_s{i}", [P, 2, 512]) for i in range(2)]
        ps_t = [pb(f"ps_t{i}", [P, 512]) for i in range(2)]
        ps_o = pb("ps_o", [P, 512])
        ps_acc = pb("ps_acc", [P, 512])

        ln = LayerNorm("ca_ln", lambda n: top.enter_context(nc.semaphore(n)), sb, JT, NT, cn["neg_half"])
        ctx_landed, res_landed, wp_landed = sem("ctx_landed"), sem("res_landed"), sem("wp_landed")
        k_stacked = [sem(f"k_stacked{m}") for m in range(KT)]
        q_stacked = [sem(f"q_stacked{i}") for i in range(2)]
        pad_zeroed = sem("pad_zeroed")
        s_psum, max_done = sem("s_psum"), sem("max_done")
        exp_done = Count(sem("exp_done"), primed=2)
        t_psum = [sem(f"t_psum{i}") for i in range(2)]
        pt_done = [Count(sem(f"pt_done{i}"), primed=1) for i in range(2)]
        inv_done, rinv_done, rinvT_done, o_psum = (sem(n) for n in ("inv_done", "rinv_done", "rinvT_done", "o_psum"))
        o_done = Count(sem("o_done"), primed=1)
        acc_psum, hi_done = sem("acc_psum"), sem("hi_done")
        acc_read = Count(sem("acc_read"), primed=1)
        f_free = Count(sem("f_free"), primed=2)
        out_stored = Count(sem("out_stored"), unit=16, primed=1)

        views = [ed_wkv[:, C * i:C * (i + 1)].rearrange("(k p) n -> p k n", p=P) for i in range(2)]
        units = [(view[:, 2 * h:2 * h + 2], w[:, :, 2 * h:2 * h + 2])
                 for view, w in zip(views, (wk, wv)) for h in range(2)]
        ws = WeightSplitter(units, stage, [sem(f"w_landed{i}") for i in range(2)], sem("w_hi"), sem("w_lo"))
        plans = {k: numbered_uses(plan_cross_attention(k)) for k in ("first", "body", "last")}

        def f_tile(name, f):
            if name == "E":
                return f32[0:TQ, f % 2, :]
            return f32[:, f % 2, 0:JP if name == "K" else JH]

        def split_dst(name, m, a, half):
            return xT[:, half, m, a, 0:JH] if name == "T" else keys[:, half, a, :]

        def run(eng, step):
            step("first", -1, plans["first"])
            with eng.Fori(0, B - 1) as b:
                step("body", b, plans["body"])
            step("last", B - 1, plans["last"])

        def bases(kind, b):
            return (0, 0, 0) if kind == "first" else (ACC0 + ACCN * b, ACC0 + FN * b, ACC0 + SPN * b)

        with nc.Block() as block:
            @block.sync
            def _(sp):
                sp.sem_inc(out_stored.sem, 16)
                ctx_tokens = lambda b: ctx_in[b].rearrange("(p t) c -> p t c", t=NT)
                tokens = lambda a, b: a[b].rearrange("(t p) c -> p t c", p=TQ)
                sp.dma_start(xs[:], ctx_tokens(0)).then_inc(ctx_landed, 16)
                ws.load(sp)
                sp.dma_start(wp[:], ed_wproj.rearrange("(k p) n -> p k n", p=P)).then_inc(wp_landed, 16)

                def stack_queries(pair, b):
                    for c, half in enumerate(STACK_Q):
                        sp.dma_start(q_stack[HD * c:HD * (c + 1), 8 * pair:8 * pair + 8, :].bitcast(F32),
                                     q2_out[b, half, 2 * pair:2 * pair + 2].rearrange(
                                         "k (j d) t -> d (k j) t", d=HD)).then_inc(q_stacked[pair], 16)

                def stack_keys(m):
                    for j in range(GH):
                        for c, half in enumerate(STACK_K):
                            sp.dma_start(k_stack[HD * c:HD * (c + 1), GH * m + j].bitcast(F32),
                                         keys[HD * j:HD * (j + 1), half].bitcast(F32)).then_inc(k_stacked[m], 16)

                def step(kind, b, items, next_x=True):
                    acc0, f0, _ = bases(kind, b)
                    if kind == "first":
                        stack_queries(0, 0)
                        stack_queries(1, 0)
                    else:
                        sp.wait_ge(out_stored.sem, out_stored.free(b))
                        sp.dma_start(res[:], tokens(res_out, b)).then_inc(res_landed, 16)
                    for name, ids, acc, f, _ in items:
                        if name == "T" and ids == (KT - 1, 1) and next_x:
                            sp.wait_ge(acc_psum, acc0 + (acc + 1))
                            sp.dma_start(xs[:], ctx_tokens(b + 2)).then_inc(ctx_landed, 16)
                        if name == "K" and ids[1] == 1:
                            sp.wait_ge(f_free.sem, f_free.done(f0 + f))
                            stack_keys(ids[0])
                        if name == "score" and ids[0] % 16 == 15 and kind == "body":
                            sp.wait_ge(s_psum, SC * b + (ids[0] + 1))
                            stack_queries(ids[0] // 16, b + 1)
                        if name == "E" and ids[0] == 1:
                            sp.wait_ge(f_free.sem, f_free.done(f0 + f))
                            sp.dma_start(tokens(out, b), res[:]).then_inc(out_stored.sem, 16)

                step("first", -1, plans["first"])
                with sp.Fori(0, B - 2) as b:
                    step("body", b, plans["body"])
                step("body", B - 2, plans["body"], next_x=False)
                step("last", B - 1, plans["last"], next_x=False)
                sp.wait_ge(out_stored.sem, out_stored.done(B - 1))

            @block.gpsimd
            def _(pool):
                pool.sem_inc(f_free.sem, 2)
                pool.memset(xT[:].bitcast(F32), 0.0).then_inc(pad_zeroed, 1)

                def step(kind, b, items):
                    acc0, f0, sp0 = bases(kind, b)
                    if kind != "last":
                        ln.inverse_root(pool, b + 1)
                    for name, ids, acc, f, s in items:
                        if name in ("T", "K"):
                            pool.wait_ge(hi_done, sp0 + (s + 1))
                            pool.tensor_tensor(split_dst(name, *ids, LO), f_tile(name, f),
                                               split_dst(name, *ids, HI).bitcast(F32), ALU.subtract)\
                                .then_inc(f_free.sem, 1)
                        if name == "E":
                            if ids[0] == 0:
                                pool.wait_ge(res_landed, 16 * b + 16)
                            pool.wait_ge(acc_read.sem, acc_read.done(acc0 + acc))
                            pool.tensor_tensor(res[:, ids[0]], f_tile(name, f), res[:, ids[0]], ALU.add)\
                                .then_inc(f_free.sem, 1)

                run(pool, step)

            @block.scalar
            def _(act):
                act.sem_inc(exp_done.sem, 2)
                act.sem_inc(pt_done[0].sem, 1)
                act.sem_inc(acc_read.sem, 1)
                for u in range(len(units)):
                    ws.round_hi(act, u)

                def step(kind, b, items):
                    acc0, f0, _ = bases(kind, b)
                    for name, ids, acc, f, _ in items:
                        m = ids[0]
                        if name == "score":
                            act.wait_ge(max_done, SC * b + (m + 1))
                            act.activation(prob[:, m % 4], ps_s[m % 2][0:TQ, :, 0:JH], ACT.Exp,
                                           bias=maxes[:, m % 4:m % 4 + 1],
                                           accum_out=sums[:, (m // GH) % 2, m % GH:m % GH + 1])\
                                .then_inc(exp_done.sem, 1)
                        if name == "probT":
                            act.wait_ge(t_psum[0], SC * b + (m + 1))
                            act.copy(probT[0:JT, (m // GH) % 2, m % GH, 0:3],
                                     ps_t[0][0:JT, 0:3 * TQ].rearrange("p (t q) -> p t q", q=TQ))\
                                .then_inc(pt_done[0].sem, 1)
                        if name not in ("V", "K", "T", "E"):
                            continue
                        act.wait_ge(acc_psum, acc0 + (acc + 1))
                        if name != "V":
                            act.wait_ge(f_free.sem, f_free.free(f0 + f))
                        if name == "T":
                            ins = act.activation(f_tile(name, f), ps_acc[:, 0:JH], ACT.Identity,
                                                 bias=cn["columns"][:, 3 * KT + m:3 * KT + m + 1],
                                                 scale=cn["columns"][:, 2 * KT + m:2 * KT + m + 1])
                        elif name == "K":
                            ins = act.copy(f_tile(name, f), ps_acc[:, 0:JP])
                        elif name == "V":
                            ins = act.copy(v[:, m], ps_acc[0:JT, :])
                        else:
                            ins = act.copy(f_tile(name, f), ps_acc[0:TQ, :])
                        ins.then_inc(acc_read.sem, 1)

                run(act, step)

            @block.vector
            def _(dve):
                dve.sem_inc(pt_done[1].sem, 1)
                dve.sem_inc(o_done.sem, 1)

                def statistics(b, tiles):
                    if tiles[0] == 0:
                        dve.wait_ge(ctx_landed, 16 * b + 16)
                    for t in tiles:
                        ln.statistics(dve, t, xs[:, t])
                    if tiles[-1] == NT - 1:
                        ln.variance(dve, b)

                def normalise(b, tiles):
                    for t in tiles:
                        ln.normalise(dve, b, t, xs[:, t], xs[:, t])

                def step(kind, b, items):
                    acc0, _, _ = bases(kind, b)
                    if kind == "first":
                        statistics(0, range(NT))
                        normalise(0, range(NT))
                        for u in range(len(units)):
                            ws.keep_lo(dve, u)
                        dve.wait_ge(pad_zeroed, 1)
                    for name, ids, acc, f, _ in items:
                        m = ids[0]
                        if name == "score":
                            dve.wait_ge(s_psum, SC * b + (m + 1))
                            dve.tensor_reduce(maxes[:, m % 4:m % 4 + 1], ps_s[m % 2][0:TQ, :, 0:JH],
                                              mybir.AxisListType.XY, ALU.max, negate=True).then_inc(max_done, 1)
                            if kind == "body" and m < 3:
                                statistics(b + 1, range(2 * m, 2 * m + 2))
                            if kind == "body" and 4 <= m < 7:
                                normalise(b + 1, range(2 * m - 8, 2 * m - 6))
                        if name == "probT":
                            u = m // GH
                            if m % GH == 2:
                                dve.wait_ge(exp_done.sem, exp_done.done(SC * b + (GH * u + GH - 1)))
                                dve.reciprocal(inv[:], sums[:, u % 2]).then_inc(inv_done, 1)
                                dve.wait_ge(inv_done, UN * b + (u + 1))
                                dve.tensor_copy(rinv[:].rearrange("p (j d) -> p j d", d=HD),
                                                inv[:].unsqueeze(2).to_broadcast([TQ, GH, HD])).then_inc(rinv_done, 1)
                            dve.wait_ge(t_psum[1], SC * b + (m + 1))
                            if m % GH == GH - 1:
                                dve.tensor_copy(rinv_T[:], ps_t[1][:, 3 * TQ:4 * TQ]).then_inc(rinvT_done, 1)
                            dve.tensor_copy(probT[0:JT, u % 2, m % GH, 3:6],
                                            ps_t[1][0:JT, 0:3 * TQ].rearrange("p (t q) -> p t q", q=TQ))\
                                .then_inc(pt_done[1].sem, 1)
                        if name == "scale":
                            q = m % 2
                            dve.wait_ge(o_psum, UN * b + (m + 1))
                            dve.wait_ge(rinvT_done, UN * b + (m + 1))
                            dve.tensor_tensor(oT[:, m // 2, TQ * q:TQ * (q + 1)], ps_o[:, TQ * q:TQ * (q + 1)],
                                              rinv_T[:], ALU.mult).then_inc(o_done.sem, 1)
                        if name == "hi":
                            what, m, a = ids
                            dve.wait_ge(acc_read.sem, acc_read.done(acc0 + acc))
                            if what == "K" and a == 0 and m > 0:
                                batch = b if m == KT - 1 else b + 1
                                dve.wait_ge(k_stacked[m - 1], STACKED_K * (batch + 1))
                            if what == "K" and a == 0 and m == 0 and kind == "body":
                                dve.wait_ge(k_stacked[KT - 1], STACKED_K * (b + 1))
                            dve.tensor_copy(split_dst(what, m, a, HI), f_tile(what, f)).then_inc(hi_done, 1)

                run(dve, step)

            @block.tensor
            def _(pe):
                ident = cn["ident"]

                def step(kind, b, items):
                    acc0, f0, _ = bases(kind, b)
                    for name, ids, acc, f, _ in items:
                        m = ids[0]
                        if name == "score":
                            g, q, h = m // 8, (m // GH) % 2, GH * (m // 8) + m % GH
                            if m % 8 == 0:
                                pe.wait_ge(k_stacked[g], STACKED_K * b + STACKED_K)
                            if m % 16 == 0:
                                pe.wait_ge(q_stacked[m // 16], STACKED_Q * b + STACKED_Q)
                            pe.wait_ge(exp_done.sem, exp_done.free(SC * b + m))
                            for a in range(2):
                                mm = pe.matmul(ps_s[m % 2][0:TQ, a, 0:JP], q_stack[:, h, TQ * q:TQ * (q + 1)],
                                               k_stack[:, h, a, :], start=True, stop=True)
                            mm.then_inc(s_psum, 1)
                        if name == "probT":
                            pe.wait_ge(exp_done.sem, exp_done.done(SC * b + m))
                            for a in range(2):
                                pe.wait_ge(pt_done[a].sem, pt_done[a].free(SC * b + m))
                                if a == 1 and m % GH == GH - 1:
                                    pe.wait_ge(rinv_done, UN * b + (m // GH + 1))
                                    pe.transpose(ps_t[1][:, 3 * TQ:4 * TQ], rinv[:], ident[0:TQ, 0:TQ])
                                for t in range(3):
                                    mm = pe.transpose(ps_t[a][0:JT, TQ * t:TQ * (t + 1)],
                                                      prob[:, m % 4, a, JT * t:JT * (t + 1)], ident[0:TQ, 0:TQ])
                                mm.then_inc(t_psum[a], 1)
                        if name == "value":
                            g, q = m // 2, m % 2
                            if m == 0:
                                last_v = acc0 + 5
                                pe.wait_ge(acc_read.sem, acc_read.done(last_v))
                            for a in range(2):
                                pe.wait_ge(pt_done[a].sem, pt_done[a].done(SC * b + (GH * m + GH - 1)))
                            pe.wait_ge(o_done.sem, o_done.free(UN * b + m))
                            for t in range(NT):
                                for j in range(GH):
                                    h = GH * g + j
                                    mm = pe.matmul(ps_o[HD * j:HD * (j + 1), TQ * q:TQ * (q + 1)],
                                                   v[:, t, HD * h:HD * (h + 1)], probT[0:JT, m % 2, j, t],
                                                   start=t == 0, stop=t == NT - 1)
                            mm.then_inc(o_psum, 1)
                        if name not in ("V", "K", "T", "E"):
                            continue
                        pe.wait_ge(acc_read.sem, acc_read.free(acc0 + acc))
                        if name == "T":
                            a = ids[1]
                            if m == 0 and a == 0:
                                pe.wait_ge(ln.xhat_done, NT * b + 2 * NT)
                            for t in range(3):
                                mm = pe.transpose(ps_acc[:, JT * t:JT * (t + 1)], xs[:, 3 * a + t, P * m:P * (m + 1)],
                                                  ident[0:JT, 0:JT])
                        elif name == "K":
                            a = ids[1]
                            if m == 0 and a == 0:
                                last_t = f0 + f - 1
                                pe.wait_ge(f_free.sem, f_free.done(last_t))
                                if kind == "first":
                                    pe.wait_ge(ws.lo_done, len(units))
                            mm = product(pe, ps_acc[:, 0:JP], lambda c, k: wk[:, c, k, P * m:P * (m + 1)],
                                         lambda c, k: xT[:, c, k, a, :])
                        elif name == "V":
                            a, t = m // 3, m % 3
                            mm = product(pe, ps_acc[0:JT, :], lambda c, k: xT[:, c, k, a, JT * t:JT * (t + 1)],
                                         lambda c, k: wv[:, c, k, :])
                        else:
                            pe.wait_ge(o_done.sem, o_done.done(UN * b + (6 + m)))
                            for g in range(KT):
                                mm = pe.matmul(ps_acc[0:TQ, :], oT[:, g, TQ * m:TQ * (m + 1)], wp[:, g, :],
                                               start=g == 0, stop=g == KT - 1)
                        mm.then_inc(acc_psum, 1)
                    if kind == "first":
                        pe.wait_ge(wp_landed, 16)

                run(pe, step)


_PRE = "L0_xattn_"
_INS = ["x", "ctx_1024", "mask_BxS_bf0"] + [_PRE + n for n in (
    "sa_wqkv", "sa_wproj", "sa_bproj", "ed_wkv", "ed_wq", "ed_wproj", "ed_bproj", "ff_w1", "ff_b1", "ff_w2", "ff_b2",
    "ln1_g", "ln1_b", "ln2_g", "ln2_b", "ln3_g", "ln3_b")]


def kernel(**inputs):
    import numpy as _np
    import concourse.bacc as _bacc
    from concourse import mybir as _mybir
    from concourse.bass_utils import run_bass_kernel_spmd as _run

    nc = _bacc.Bacc("TRN2", target_bir_lowering=False, num_devices=1)
    arrays, args = {}, []
    for name in _INS:
        a = _np.ascontiguousarray(inputs[name])
        arrays[f"in_{name}_dram"] = a
        args.append(nc.dram_tensor(f"in_{name}_dram", a.shape, _mybir.dt.from_np(a.dtype), kind="ExternalInput").ap())
    out = nc.dram_tensor("out_0_dram", inputs["x"].shape, _mybir.dt.float32, kind="ExternalOutput").ap()
    xattn_kernel(nc, *args, out)
    r = _run(nc, [arrays], core_ids=[0])
    return r.results[0]["out_0_dram"]
```

```python
from contextlib import ExitStack

import concourse.bass as bass
from concourse import mybir

ALU = mybir.AluOpType
ACT = mybir.ActivationFunctionType
AX_X = mybir.AxisListType.X
F32 = mybir.dt.float32
F32R = mybir.dt.float32r
U8 = mybir.dt.uint8

P = 128
LN_EPS = 1e-5
CTX_TILES = 6
MASKED = -1e30

HI, LO = 0, 1
PASSES = ((HI, HI), (HI, LO), (LO, HI))


class Count:

    def __init__(self, sem, unit=1, primed=0):
        self.sem, self.unit, self.primed = sem, unit, primed

    def done(self, n):
        return (n + (1 + self.primed)) * self.unit

    def free(self, n):
        return (n + 1) * self.unit



class WeightSplitter:

    def __init__(self, units, stage, landed, hi_done, lo_done):
        self.units, self.stage, self.landed = units, stage, landed
        self.hi_done, self.lo_done = hi_done, lo_done

    def load(self, sp, first=0, last=None):
        depth = len(self.stage)
        for n, (src, _) in list(enumerate(self.units))[first:last]:
            if n >= depth:
                sp.wait_ge(self.lo_done, n - depth + 1)
            sp.dma_start(self.stage[n % depth], src).then_inc(self.landed[n % depth], 16)

    def round_hi(self, act, n):
        depth = len(self.stage)
        act.wait_ge(self.landed[n % depth], 16 * (n // depth + 1))
        act.copy(self.units[n][1][:, HI], self.stage[n % depth]).then_inc(self.hi_done, 1)

    def keep_lo(self, dve, n):
        dve.wait_ge(self.hi_done, n + 1)
        dve.tensor_tensor(self.units[n][1][:, LO], self.stage[n % len(self.stage)],
                          self.units[n][1][:, HI].bitcast(F32), ALU.subtract).then_inc(self.lo_done, 1)


def weight_halves(src, dst):
    src = src.rearrange("(k p) n -> p k n", p=P)
    return [(src[:, 2 * h:2 * h + 2], dst[:, :, 2 * h:2 * h + 2]) for h in range(2)]


class LayerNorm:

    def __init__(self, name, sem, sb, part, tiles, neg_half):
        self.part, self.tiles, self.neg_half = part, tiles, neg_half
        self.stats = sb(f"{name}_stats", [part, tiles + 1, 6], F32)
        self.mean_var = sb(f"{name}_mean_var", [part, tiles, 2], F32)
        self.var_eps = sb(f"{name}_var_eps", [part, tiles], F32)
        self.rstd = sb(f"{name}_rstd", [part, tiles], F32)
        self.stats_done = sem(f"{name}_stats_done")
        self.aggr_done = sem(f"{name}_aggr_done")
        self.eps_done = sem(f"{name}_eps_done")
        self.rstd_done = sem(f"{name}_rstd_done")
        self.xhat_done = sem(f"{name}_xhat_done")

    def statistics(self, dve, t, src):
        dve.bn_stats(self.stats[:, t, :], src).then_inc(self.stats_done, 1)

    def variance(self, dve, r):
        n = self.tiles
        dve.wait_ge(self.stats_done, r * n + n)
        dve.memset(self.stats[:, n, :], 0.0)
        for t in range(n):
            dve.bn_aggr(self.mean_var[:, t, :], self.stats[:, t, :]).then_inc(self.aggr_done, 1)
        dve.wait_ge(self.aggr_done, r * n + n)
        dve.tensor_scalar(self.var_eps[:], self.mean_var[:, :, 1], LN_EPS, None, ALU.add).then_inc(self.eps_done, 1)

    def inverse_root(self, pool, r):
        pool.wait_ge(self.eps_done, r + 1)
        pool.tensor_tensor(self.rstd[:], self.var_eps[:], self.neg_half[0:self.part, 0:self.tiles],
                           ALU.pow).then_inc(self.rstd_done, 1)

    def normalise(self, dve, r, t, src, dst):
        if t == 0:
            dve.wait_ge(self.rstd_done, r + 1)
        dve.tensor_scalar(dst, src, self.mean_var[:, t, 0:1], self.rstd[:, t:t + 1],
                          ALU.subtract, ALU.mult).then_inc(self.xhat_done, 1)


def split_exactly(pool, one, hi, lo, src, hi_done, count):
    pool.tensor_tensor(hi, src, one[:].to_broadcast(list(src.shape)), ALU.mult).then_inc(hi_done, 1)
    pool.wait_ge(hi_done, count)
    return pool.tensor_tensor(lo, src, hi.bitcast(F32), ALU.subtract)


def product(pe, acc, lhs, rhs):
    steps = [(k, a, b) for k in range(4) for a, b in PASSES]
    for n, (k, a, b) in enumerate(steps):
        mm = pe.matmul(acc, lhs(a, k), rhs(b, k), start=n == 0, stop=n == len(steps) - 1)
    return mm


def feed_forward(nc, top, cn, x, ff_w1, ff_b1, ff_w2, ff_b2, ed_bproj, ln_params, ffn_out):
    B, T, C = x.shape
    FF = ff_w1.shape[1]
    KT, HT, CH = C // P, FF // P, FF // C
    TOK = 2 * P
    GROUPS = B * T // TOK
    x_rows = x.rearrange("b t c -> (b t) c").rearrange("(g t p) c -> g p t c", t=2, p=P)
    ffn_rows = ffn_out.rearrange("(g t p) c -> g p t c", t=2, p=P)

    with ExitStack() as ph:
        def sem(name):
            return top.enter_context(nc.semaphore("ff_" + name))

        def sb(name, shape, dt):
            return ph.enter_context(nc.sbuf_tensor("ff_" + name, shape, dt))

        def pb(name, shape):
            return ph.enter_context(nc.psum_tensor("ff_" + name, shape, F32))

        w1 = [sb(f"w1_{c}", [P, 2, KT, C], F32R) for c in range(CH)]
        w2 = [sb(f"w2_{c}", [P, 2, KT, C], F32R) for c in range(CH)]
        stage = [sb(f"stage{i}", [P, 2, C], F32)[:] for i in range(3)]
        xin = sb("xin", [P, 2, C], F32)
        xhat = sb("xhat", [P, 2, C], F32)
        xaff = sb("xaff", [P, KT, TOK], F32)
        xT = sb("xT", [P, 2, KT, TOK], F32R)
        hrelu = sb("hrelu", [P, 2, TOK], F32)
        hT = sb("hT", [P, 2, HT, TOK], F32R)
        y = sb("y", [P, 2, C], F32)
        bias = sb("bias", [P, 2, C], F32)
        vec_rows = sb("vec_rows", [6 * KT + HT, P], F32)
        b1 = cn["columns"][:, 6 * KT:]
        ps_x = pb("ps_x", [P, KT, TOK])
        ps_h = [pb(f"ps_h{i}", [P, 512]) for i in range(2)]
        ps_y = [pb(f"ps_y{i}", [P, 512]) for i in range(2)]

        x_landed, bias_landed = sem("x_landed"), sem("bias_landed")
        ln = LayerNorm("ff_ln", lambda n: top.enter_context(nc.semaphore(n)), sb, P, 2, cn["neg_half"])
        xT_psum, xaff_ready = sem("xT_psum"), sem("xaff_ready")
        xhi_ready, xlo_ready = sem("xhi_ready"), sem("xlo_ready")
        h_psum, y_psum = sem("h_psum"), sem("y_psum")
        relu_done = Count(sem("relu_done"), primed=2)
        hhi_done = sem("hhi_done")
        hlo_done = Count(sem("hlo_done"), primed=2)
        y_done = Count(sem("y_done"), primed=2)
        y_stored = [Count(sem(f"y_stored{t}"), unit=16, primed=1) for t in range(2)]
        bias_ready, vec_landed, vec_psum, columns_ready = (
            sem(n) for n in ("bias_ready", "vec_landed", "vec_psum", "columns_ready"))
        w1_v = ff_w1.rearrange("(k p) (c n) -> c p k n", p=P, n=C)
        w2_v = ff_w2.rearrange("(c k p) n -> c p k n", k=KT, p=P)
        units = [(v[c][:, 2 * h:2 * h + 2], w[c][:, :, 2 * h:2 * h + 2])
                 for v, w in ((w1_v, w1), (w2_v, w2)) for c in range(CH) for h in range(2)]
        ws = WeightSplitter(units, stage, [sem(f"w_landed{i}") for i in range(3)], sem("w_hi"), sem("w_lo"))

        with nc.Block() as block:
            @block.sync
            def _(sp):
                for t in range(2):
                    sp.sem_inc(y_stored[t].sem, 16)
                sp.dma_start(xin[:], x_rows[0]).then_inc(x_landed, 16)
                ws.load(sp, 0, 2)
                for n, v in enumerate(ln_params):
                    sp.dma_start(vec_rows[KT * n:KT * (n + 1), :], v.rearrange("(k p) -> k p", p=P)).then_inc(vec_landed, 16)
                sp.dma_start(vec_rows[6 * KT:, :], ff_b1.rearrange("(m p) -> m p", p=P)).then_inc(vec_landed, 16)
                sp.dma_start(bias[:, 0], ff_b2.partition_broadcast(P)).then_inc(bias_landed, 16)
                sp.dma_start(bias[:, 1], ed_bproj.partition_broadcast(P)).then_inc(bias_landed, 16)
                ws.load(sp, 2)

                def group(g, last):
                    if not last:
                        sp.wait_ge(ln.xhat_done, 2 * g + 2)
                        sp.dma_start(xin[:], x_rows[g + 1]).then_inc(x_landed, 16)
                    for t in range(2):
                        sp.wait_ge(y_done.sem, y_done.done(2 * g + t))
                        sp.dma_start(ffn_rows[g][:, t], y[:, t]).then_inc(y_stored[t].sem, 16)

                with sp.Fori(0, GROUPS - 1) as g:
                    group(g, False)
                group(GROUPS - 1, True)
                for t in range(2):
                    sp.wait_ge(y_stored[t].sem, y_stored[t].done(GROUPS - 1))

            @block.gpsimd
            def _(pool):
                pool.sem_inc(hlo_done.sem, 2)
                ident, ready = cn["ident"], cn["ident_ready"]
                pool.memset(ident[:], 0.0).then_inc(ready, 1)
                pool.wait_ge(ready, 1)
                pool.affine_select(out=ident[:], in_=ident[:], compare_op=ALU.not_equal, fill=1.0, base=0,
                                   pattern=[[-1, P]], channel_multiplier=1).then_inc(ready, 1)
                pool.memset(cn["neg_half"][:], -0.5).then_inc(ready, 1)
                pool.memset(cn["one"][:], 1.0).then_inc(ready, 1)
                pool.wait_ge(ready, 4)

                def prepare(g):
                    ln.inverse_root(pool, g)
                    pool.wait_ge(xhi_ready, g + 1)
                    pool.tensor_tensor(xT[:, LO], xaff[:], xT[:, HI].bitcast(F32),
                                       ALU.subtract).then_inc(xlo_ready, 1)

                def group(g, last):
                    for m in range(HT):
                        pool.wait_ge(hhi_done, g * HT + m + 1)
                        pool.tensor_tensor(hT[:, LO, m], hrelu[:, m % 2], hT[:, HI, m].bitcast(F32),
                                           ALU.subtract).then_inc(hlo_done.sem, 1)
                    if not last:
                        prepare(g + 1)

                prepare(0)
                with pool.Fori(0, GROUPS - 1) as g:
                    group(g, False)
                group(GROUPS - 1, True)

            @block.scalar
            def _(act):
                act.sem_inc(relu_done.sem, 2)

                def prepare(g):
                    for k in range(KT):
                        act.wait_ge(xT_psum, g * KT + (k | 1) + 1)
                        act.activation(xaff[:, k], ps_x[:, k], ACT.Identity, bias=cn["columns"][:, 5 * KT + k:5 * KT + k + 1],
                                       scale=cn["columns"][:, 4 * KT + k:4 * KT + k + 1]).then_inc(xaff_ready, 1)

                def group(g, last, weights=False):
                    for m in range(HT):
                        if weights and m % KT == 0 and m < HT - KT:
                            for u in (0, 1):
                                ws.round_hi(act, m // 2 + 2 + u)
                        act.wait_ge(h_psum, g * HT + m + 1)
                        act.wait_ge(hlo_done.sem, hlo_done.free(g * HT + m))
                        act.activation(hrelu[:, m % 2], ps_h[m % 2][:, 0:TOK], ACT.Relu,
                                       bias=b1[:, m:m + 1]).then_inc(relu_done.sem, 1)
                    if weights:
                        for u in range(2 * CH, len(units)):
                            ws.round_hi(act, u)
                    if not last:
                        prepare(g + 1)

                act.wait_ge(vec_psum, 1)
                act.copy(cn["columns"][:], ps_h[0][:, 0:6 * KT + HT]).then_inc(columns_ready, 1)
                act.wait_ge(columns_ready, 1)
                for u in range(2):
                    ws.round_hi(act, u)
                prepare(0)
                group(0, False, weights=True)
                with act.Fori(1, GROUPS - 1) as g:
                    group(g, False)
                group(GROUPS - 1, True)

            @block.vector
            def _(dve):
                dve.sem_inc(y_done.sem, 2)

                def normalise(g):
                    dve.wait_ge(x_landed, 16 * g + 16)
                    for t in range(2):
                        ln.statistics(dve, t, xin[:, t])
                    ln.variance(dve, g)
                    for t in range(2):
                        ln.normalise(dve, g, t, xin[:, t], xhat[:, t])

                def tokens_hi(g):
                    dve.wait_ge(xaff_ready, KT * g + KT)
                    dve.tensor_copy(xT[:, HI], xaff[:]).then_inc(xhi_ready, 1)

                def result(g, t):
                    dve.wait_ge(y_psum, 2 * g + t + 1)
                    dve.wait_ge(y_stored[t].sem, y_stored[t].free(g))
                    dve.tensor_tensor(y[:, t], ps_y[t][:], bias[:, 0], ALU.add).then_inc(y_done.sem, 1)

                def group(g, last, weights=False):
                    for m in range(HT):
                        if weights and m % KT == 0 and m < HT - KT:
                            for u in (0, 1):
                                ws.keep_lo(dve, m // 2 + 2 + u)
                        dve.wait_ge(relu_done.sem, relu_done.done(g * HT + m))
                        dve.tensor_copy(hT[:, HI, m], hrelu[:, m % 2]).then_inc(hhi_done, 1)
                    if weights:
                        for u in range(2 * CH, len(units)):
                            ws.keep_lo(dve, u)
                    if not last:
                        normalise(g + 1)
                    result(g, 0)
                    if not last:
                        tokens_hi(g + 1)
                    result(g, 1)

                normalise(0)
                for u in range(2):
                    ws.keep_lo(dve, u)
                dve.wait_ge(bias_landed, 32)
                dve.tensor_tensor(bias[:, 0], bias[:, 0], bias[:, 1], ALU.add).then_inc(bias_ready, 1)
                tokens_hi(0)
                dve.wait_ge(bias_ready, 1)
                group(0, False, weights=True)
                with dve.Fori(1, GROUPS - 1) as g:
                    group(g, False)
                group(GROUPS - 1, True)

            @block.tensor
            def _(pe):
                def transposes(g):
                    for k in range(KT):
                        for t in range(2):
                            if k == 0:
                                pe.wait_ge(ln.xhat_done, 2 * g + t + 1)
                            mm = pe.transpose(ps_x[:, k, P * t:P * (t + 1)], xhat[:, t, P * k:P * (k + 1)],
                                              cn["ident"][:])
                        mm.then_inc(xT_psum, 1)

                def hidden(g, weights=False):
                    pe.wait_ge(xlo_ready, g + 1)
                    for m in range(HT):
                        c, n = m // KT, m % KT
                        if weights and n == 0:
                            pe.wait_ge(ws.lo_done, 2 * c + 2)
                        pe.wait_ge(relu_done.sem, relu_done.free(g * HT + m))
                        product(pe, ps_h[m % 2][:, 0:TOK], lambda a, k: w1[c][:, a, k, P * n:P * (n + 1)],
                                lambda b, k: xT[:, b, k, :]).then_inc(h_psum, 1)

                def result(g, t, weights=False):
                    pe.wait_ge(y_done.sem, y_done.free(2 * g + t))
                    for c in range(CH):
                        if weights:
                            pe.wait_ge(ws.lo_done, 2 * CH + 2 * c + 2)
                        for k in range(KT):
                            m = c * KT + k
                            for a, b in PASSES:
                                mm = pe.matmul(ps_y[t][:], hT[:, a, m, P * t:P * (t + 1)], w2[c][:, b, k, :],
                                               start=(m == 0 and (a, b) == PASSES[0]),
                                               stop=(m == HT - 1 and (a, b) == PASSES[-1]))
                    mm.then_inc(y_psum, 1)

                def group(g, last, weights=False):
                    hidden(g, weights)
                    pe.wait_ge(hlo_done.sem, hlo_done.done(g * HT + HT - 1))
                    result(g, 0, weights)
                    if not last:
                        transposes(g + 1)
                    result(g, 1)

                pe.wait_ge(cn["ident_ready"], 4)
                pe.wait_ge(vec_landed, 16 * 7)
                pe.transpose(ps_h[0][:, 0:6 * KT + HT], vec_rows[:], cn["ident"][0:6 * KT + HT, 0:6 * KT + HT])\
                    .then_inc(vec_psum, 1)
                pe.wait_ge(columns_ready, 1)
                transposes(0)
                group(0, False, weights=True)
                with pe.Fori(1, GROUPS - 1) as g:
                    group(g, False)
                group(GROUPS - 1, True)


def xattn_kernel(nc, x, ctx_in, mask, wqkv, wproj, bproj, ed_wkv, ed_wq, ed_wproj, ed_bproj,
                 ff_w1, ff_b1, ff_w2, ff_b2, ln1_g, ln1_b, ln2_g, ln2_b, ln3_g, ln3_b, out):
    B, T, C = x.shape
    FF = ff_w1.shape[1]
    KT = C // P
    ffn_out = nc.dram_tensor("ffn_out", (B * T, C), F32, kind="Internal").ap()
    res_out = nc.dram_tensor("res_out", (B, T, C), F32, kind="Internal").ap()
    qk_rows = nc.dram_tensor("qk_rows", (B, 2, 2, C, T), F32, kind="Internal").ap()
    q2_out = nc.dram_tensor("q2_out", (B, 2, KT, P, T), F32, kind="Internal").ap()
    with ExitStack() as top:
        cn = {
            "ident": top.enter_context(nc.sbuf_tensor("ident", [P, P], F32)),
            "columns": top.enter_context(nc.sbuf_tensor("columns", [P, 6 * KT + FF // P], F32)),
            "one": top.enter_context(nc.sbuf_tensor("one", [P, 1], F32)),
            "neg_half": top.enter_context(nc.sbuf_tensor("neg_half", [P, 8], F32)),
            "ident_ready": top.enter_context(nc.semaphore("ident_ready")),
        }
        feed_forward(nc, top, cn, x, ff_w1, ff_b1, ff_w2, ff_b2, ed_bproj,
                     (ln1_g, ln1_b, ln2_g, ln2_b, ln3_g, ln3_b), ffn_out)
        w_first = top.enter_context(nc.sbuf_tensor("w_first", [P, 2, KT, C], F32R))
        ctx_tokens = top.enter_context(nc.sbuf_tensor("ctx_tokens", [P, CTX_TILES, C], F32))
        ctx_landed = top.enter_context(nc.semaphore("ctx_landed"))
        self_attention(nc, top, cn, w_first, ctx_tokens, ctx_landed, ctx_in, x, mask, wqkv, wproj, bproj, ed_wq, ed_wkv, ffn_out, qk_rows, res_out,
                       q2_out)
        cross_attention(nc, top, cn, w_first, ctx_tokens, ctx_landed, ctx_in, ed_wkv, ed_wproj, res_out, q2_out, out)


POOL_SPLITS = "QKY"


def plan_self_attention(kind):
    if kind == "first":
        return [("T", 0), ("split", "T", 0), ("T", 1), ("split", "T", 1)] + \
            [(n, 2 * pair + m) for pair in range(2) for n in "QK" for m in range(2)] + [("V", 0)]
    if kind == "final":
        return [("R", 0), ("split", "R", 0), ("R", 1), ("split", "R", 1)] + [("Y", m) for m in range(4)]
    fill = {0: ("V", 1), 1: ("R", 0), 2: ("R", 1), 3: ("T", 0), 4: ("T", 1), 5: ("Y", 0), 6: ("Q", 0), 7: ("Q", 1),
            8: ("Y", 1),
            9: ("Q", 2), 10: ("Q", 3), 11: ("Y", 2), 12: ("K", 0), 13: ("K", 1), 14: ("Y", 3), 15: ("K", 2),
            17: ("K", 3)}
    items, late = [], []
    for i in range(19):
        if i < 16:
            items.append(("score", i))
        if i >= 3:
            items.append(("probT", i - 3))
        if i < 16:
            items.append(("exp", i))
        items += late
        late = []
        if i >= 7 and i % 4 == 3:
            items.append(("value", (i - 7) // 4))
            late.append(("scale", items[-1][1]))
        t = fill.get(i)
        if t and not (t[0] in "RY" and kind == "body0") and not (t[0] in "TQK" and kind == "last"):
            items.append(t)
            if t[0] in "TR":
                late.append(("split",) + t)
    return items + [("value", 3)] + [("V", 0)] * (kind != "last") + [("scale", 3), ("P", 0), ("P", 1)]


def numbered(plan):
    counts, out, seen = [0, 0, 0, 0], [], {}
    for item in plan:
        if item[0] == "split":
            out.append(("split", item[1:], *seen[item[1:]]))
            continue
        seen[item] = tuple(counts)
        out.append((item[0], item[1:], *counts))
        if item[0] in "TQKVPRYE":
            for n, counted in enumerate((True, item[0] != "V", item[0] in POOL_SPLITS, item[0] in "TR")):
                counts[n] += counted
    return out, tuple(counts)


class Plans:

    def __init__(self, plan, batches, kinds):
        self.batches, self.kinds = batches, kinds
        self.items, self.uses = {}, {}
        for kind in kinds:
            self.items[kind], (acc, f32, pool, dve) = numbered(plan(kind))
            self.uses[kind] = acc, f32 // 2, pool, dve

    def bases(self, kind, b):
        u = self.uses
        if kind == "first":
            return 0, 0, 0, 0
        if kind == "body0":
            return u["first"]
        if kind == "final":
            return tuple(n + m for n, m in zip(self.bases("last", b - 1), u["last"]))
        return tuple(f + o - n + n * b for f, o, n in zip(u["first"], u["body0"], u["body"]))

    def run(self, eng, step):
        step("first", -1, self.items["first"])
        step("body0", 0, self.items["body0"])
        with eng.Fori(1, self.batches - 1) as b:
            step("body", b, self.items["body"])
        step("last", self.batches - 1, self.items["last"])
        if "final" in self.kinds:
            step("final", self.batches, self.items["final"])


class TwoTiles:

    def __init__(self, sems):
        self.sems = sems

    def sem(self, n):
        return self.sems[n % 2]

    def wait_free(self, eng, pairs, n):
        eng.wait_ge(self.sems[n % 2], pairs + (n // 2 + 1))

    def wait_done(self, eng, pairs, n):
        eng.wait_ge(self.sems[n % 2], pairs + (n // 2 + 2))


def self_attention(nc, top, cn, w_first, ctx_tokens, ctx_landed, ctx_in, x, mask, wqkv, wproj, bproj, ed_wq, ed_wkv, ffn_out, qk_rows, res_out,
                   q2_out):
    B, T, C = x.shape
    KT = C // P
    H, HD, GH = 16, 32, 4
    TQ = T // 2
    SCALE = float(C) ** -0.5
    STACK_Q, STACK_K = (HI, LO, HI), (HI, HI, LO)
    KS = 3 * HD
    STACKED = 16 * 2 * 3

    with ExitStack() as ph:
        def sem(name):
            return top.enter_context(nc.semaphore("sa_" + name))

        def sb(name, shape, dt):
            return ph.enter_context(nc.sbuf_tensor("sa_" + name, shape, dt))

        def pb(name, shape):
            return ph.enter_context(nc.psum_tensor("sa_" + name, shape, F32))

        w = {n: sb(f"w_{n}", [P, 2, KT, C], F32R) for n in "kvpy"}
        w["q"] = w_first
        xin_t, xhat_t, rhat_t = (ctx_tokens[:, 2 * i:2 * i + 2] for i in range(3))
        xin = xin_t[0:TQ]
        xhat = xhat_t[0:TQ]
        rhat = rhat_t[0:TQ]
        res = sb("res", [TQ, 2, C], F32)
        fin = sb("fin", [TQ, 2, C], F32)
        bias = sb("bias", [TQ, C], F32)
        xT = sb("xT", [P, 2, KT, T], F32R)
        rT = sb("rT", [P, 2, KT, T], F32R)
        f32 = sb("f32", [P, 2, C], F32)
        qT = sb("qT", [P, 2, KT, T], F32R)
        kT = sb("kT", [P, 2, KT, T], F32R)
        q_stack = sb("q_stack", [KS, H, T], F32R)
        k_stack = sb("k_stack", [KS, H, T], F32R)
        v = sb("v", [TQ, 2, C], F32)
        prob = sb("prob", [TQ, 4, TQ + T], F32)
        probT = sb("probT", [P, 8, T + TQ], F32)
        maxes = sb("maxes", [TQ, 4, 2], F32)
        sums = sb("sums", [TQ, 2, 2, GH], F32)
        inv = sb("inv", [TQ, 2, GH], F32)
        rinv = sb("rinv", [TQ, 2, 2, P], F32)
        rinv_T = sb("rinv_T", [P, 2, T], F32)
        of = sb("of", [P, 2, T], F32)
        oT = sb("oT", [P, 2, KT, T], F32R)
        yT = sb("yT", [P, 2, KT, T], F32R)
        mask_u8 = sb("mask_u8", [TQ, T], U8)
        mask_f = sb("mask_f", [TQ, T], F32)
        causal = sb("causal", [TQ, 2, T], F32)
        masks = sb("masks", [TQ, 2, T], F32R)
        ident_r = sb("ident_r", [TQ, TQ], F32R)
        ps_s = [pb(f"ps_s{i}", [P, 512]) for i in range(2)]
        ps_t = [pb(f"ps_t{i}", [P, 512]) for i in range(2)]
        ps_o = [pb(f"ps_o{i}", [P, 512]) for i in range(2)]
        ps_acc = [pb(f"ps_acc{i}", [P, 512]) for i in range(2)]

        mk_sem = lambda n: top.enter_context(nc.semaphore(n))
        ln1 = LayerNorm("sa_ln1", mk_sem, sb, TQ, 2, cn["neg_half"])
        ln2 = LayerNorm("sa_ln2", mk_sem, sb, TQ, 2, cn["neg_half"])
        x_landed, mask_landed, res_landed, fin_landed, bias_landed = (
            sem(n) for n in ("x_landed", "mask_landed", "res_landed", "fin_landed", "bias_landed"))
        rows_written = [sem(f"rows_written{m}") for m in range(KT)]
        stacked = [sem(f"stacked{i}") for i in range(2)]
        causal_ready, mask_ready, masks_ready, bias_added, ident_rounded = (
            sem(n) for n in ("causal_ready", "mask_ready", "masks_ready", "bias_added", "ident_rounded"))
        s_psum, max_done, inv_done, recip_done = (sem(n) for n in ("s_psum", "max_done", "inv_done", "recip_done"))
        exp_done = Count(sem("exp_done"), primed=2)
        t_psum, o_psum, rinvT_done, ohi_done = (sem(n) for n in ("t_psum", "o_psum", "rinvT_done", "ohi_done"))
        probT_done = Count(sem("probT_done"), primed=2)
        of_done = Count(sem("of_done"), primed=2)
        olo_done = Count(sem("olo_done"), primed=2)
        acc_psum = sem("acc_psum")
        acc_read = Count(sem("acc_read"), primed=2)
        hi_done, thi_done = sem("hi_done"), sem("thi_done")
        f_free = TwoTiles([sem(f"f_free{i}") for i in range(2)])
        fin_done = sem("fin_done")
        res_stored = Count(sem("res_stored"), unit=16, primed=1)
        y_stored = Count(sem("y_stored"), unit=32, primed=1)

        w_views = {"q": wqkv[:, 0:C], "k": wqkv[:, C:2 * C], "v": wqkv[:, 2 * C:3 * C], "p": wproj, "y": ed_wq}
        units = [u for n in "qkvpy" for u in weight_halves(w_views[n], w[n])]
        stage_t = probT[:].rearrange("p a b -> p (a b)")
        stage = [stage_t[:, 2 * C * i:2 * C * (i + 1)].rearrange("p (k n) -> p k n", k=2) for i in range(2)]
        ws = WeightSplitter(units, stage + [rhat_t], [sem(f"w_landed{i}") for i in range(3)], sem("w_hi"),
                            sem("w_lo"))
        ws_next = WeightSplitter(weight_halves(ed_wkv[:, 0:C], w_first), [xin_t, xhat_t],
                                 [sem(f"wk_landed{i}") for i in range(2)], sem("wk_hi"), sem("wk_lo"))
        weights_before = {("T", 0): (0, 1), ("Q", 0): (2, 3), ("Q", 2): (4, 5)}
        plans = Plans(plan_self_attention, B, ("first", "body0", "body", "last", "final"))
        bases = plans.bases

        def f_tile(name, f):
            if name in ("T", "R"):
                return f32[:, f % 2, 0:2 * T].rearrange("p (k t) -> p k t", k=2)
            if name == "P":
                return f32[0:TQ, f % 2, :]
            return f32[:, f % 2, 0:T]

        def split_dst(name, m, half):
            if name in ("T", "R"):
                return (xT if name == "T" else rT)[:, half, 2 * m:2 * m + 2, :]
            return {"Q": qT, "K": kT, "Y": yT}[name][:, half, m, :]

        with nc.Block() as block:
            @block.sync
            def _(sp):
                sp.sem_inc(res_stored.sem, 16)
                sp.sem_inc(y_stored.sem, 32)
                tokens = lambda a, b: a[b].rearrange("(t p) c -> p t c", p=TQ)
                ffn_tokens = ffn_out.rearrange("(b t) c -> b t c", b=B)
                mask_row = lambda b: mask[b].partition_broadcast(TQ)
                sp.dma_start(xin[:], tokens(x, 0)).then_inc(x_landed, 16)
                sp.dma_start(mask_u8[:], mask_row(0)).then_inc(mask_landed, 16)
                sp.dma_start(bias[:], bproj.partition_broadcast(TQ)).then_inc(bias_landed, 16)
                ws.load(sp)

                def write_rows(name, m, f, b, f0):
                    f_free.wait_done(sp, f0, f)
                    src, dst = (qT, qk_rows[b + 1, 0]) if name == "Q" else (kT, qk_rows[b + 1, 1])
                    sp.dma_start(dst[:, P * m:P * (m + 1)].rearrange("a p t -> p a t"), src[:, :, m, :].bitcast(F32))\
                        .then_inc(rows_written[m], 16)

                def stack(kind, pair, b):
                    if kind != "first":
                        sp.wait_ge(s_psum, 16 * b + (8 * pair + 8))
                    for m in (2 * pair, 2 * pair + 1):
                        sp.wait_ge(rows_written[m], 32 * b + 64)
                    heads = slice(8 * pair, 8 * pair + 8)
                    for i, (dst, order) in enumerate(((q_stack, STACK_Q), (k_stack, STACK_K))):
                        for c, half in enumerate(order):
                            sp.dma_start(
                                dst[HD * c:HD * (c + 1), heads, :].bitcast(F32),
                                qk_rows[b + 1, i, half, 2 * P * pair:2 * P * (pair + 1)].rearrange(
                                    "(h d) t -> d h t", d=HD)).then_inc(stacked[pair], 16)

                def step(kind, b, items, next_x=True):
                    _, f0, _, _ = bases(kind, b)
                    if kind == "first":
                        sp.wait_ge(ln1.xhat_done, 2)
                        sp.dma_start(xin[:], tokens(x, 1)).then_inc(x_landed, 16)
                        sp.wait_ge(mask_ready, 1)
                        sp.dma_start(mask_u8[:], mask_row(1)).then_inc(mask_landed, 16)
                    if kind not in ("first", "body0"):
                        sp.wait_ge(fin_done, b)
                        sp.dma_start(tokens(res_out, b + -1), fin[:]).then_inc(res_stored.sem, 16)
                        if kind == "body":
                            sp.dma_start(mask_u8[:], mask_row(b + 1)).then_inc(mask_landed, 16)
                    if kind not in ("first", "final"):
                        if kind != "body0":
                            sp.wait_ge(ln2.xhat_done, 2 * b)
                        sp.dma_start(res[:], tokens(x, b)).then_inc(res_landed, 16)
                        sp.wait_ge(res_stored.sem, res_stored.free(b))
                        sp.dma_start(fin[:], tokens(ffn_tokens, b)).then_inc(fin_landed, 16)
                    if kind == "last":
                        f_free.wait_done(sp, f0, -1)
                        ws_next.load(sp)
                    for name, ids, acc, f, _, _ in items:
                        m = ids[0]
                        if name == "T" and m == 1 and next_x and kind != "first":
                            sp.wait_ge(ln1.xhat_done, 2 * b + 4)
                            sp.dma_start(xin[:], tokens(x, b + 2)).then_inc(x_landed, 16)
                        if name in ("Q", "K"):
                            write_rows(name, m, f, b, f0)
                            if name == "K" and m % 2 == 1:
                                stack(kind, m // 2, b)
                        if kind == "final" and (name, m) == ("R", 1):
                            f_free.wait_done(sp, f0, f)
                            sp.dma_start(ctx_tokens[0:ctx_in.shape[1] // CTX_TILES], ctx_in[0].rearrange(
                                "(p t) c -> p t c", t=CTX_TILES)).then_inc(ctx_landed, 16)
                        if name == "Y" and m == KT - 1:
                            f_free.wait_done(sp, f0, f)
                            for half in (HI, LO):
                                sp.dma_start(q2_out[b + -1, half].rearrange("k p t -> p k t"),
                                             yT[:, half].bitcast(F32)).then_inc(y_stored.sem, 16)

                step("first", -1, plans.items["first"])
                step("body0", 0, plans.items["body0"])
                with sp.Fori(1, B - 2) as b:
                    step("body", b, plans.items["body"])
                step("body", B - 2, plans.items["body"], next_x=False)
                step("last", B - 1, plans.items["last"], next_x=False)
                step("final", B, plans.items["final"], next_x=False)
                sp.wait_ge(res_stored.sem, res_stored.done(B - 1))
                sp.wait_ge(y_stored.sem, y_stored.done(B - 1))
                sp.wait_ge(ctx_landed, 16)

            @block.gpsimd
            def _(pool):
                for tile in range(2):
                    pool.sem_inc(f_free.sems[tile], 1)
                pool.memset(causal[:], 0.0).then_inc(causal_ready, 1)
                pool.wait_ge(causal_ready, 1)
                pool.affine_select(out=causal[:], in_=causal[:], compare_op=ALU.is_ge, fill=MASKED, base=0,
                                   pattern=[[TQ, 2], [-1, T]], channel_multiplier=1).then_inc(causal_ready, 1)

                def step(kind, b, items):
                    acc0, f0, sp0, _ = bases(kind, b)
                    if kind not in ("last", "final"):
                        ln1.inverse_root(pool, b + 1)
                    for name, ids, acc, f, s, _ in items:
                        m = ids[0]
                        if name in ("Q", "K", "Y"):
                            pool.wait_ge(acc_read.sem, acc_read.done(acc0 + acc))
                            if kind != "first" and name in ("Q", "K"):
                                pool.wait_ge(rows_written[m], 32 * b + 32)
                            if name == "Y" and m == 0:
                                pool.wait_ge(y_stored.sem, y_stored.free(b + -1))
                            split_exactly(pool, cn["one"], split_dst(name, m, HI), split_dst(name, m, LO),
                                          f_tile(name, f), hi_done, sp0 + (s + 1)).then_inc(f_free.sem(f), 1)
                        if name == "P" and m == 1:
                            ln2.inverse_root(pool, b)

                plans.run(pool, step)

            @block.scalar
            def _(act):
                act.sem_inc(acc_read.sem, 2)
                act.sem_inc(exp_done.sem, 2)

                def step(kind, b, items):
                    acc0, f0, _, _ = bases(kind, b)
                    if kind == "body0":
                        for u in range(6, len(units)):
                            ws.round_hi(act, u)
                    for name, ids, acc, f, _, _ in items:
                        m = ids[0]
                        if kind == "first" and (name, m) in weights_before:
                            for u in weights_before[name, m]:
                                ws.round_hi(act, u)
                        if name == "exp":
                            act.wait_ge(max_done, 16 * b + (m + 1))
                            for q in range(2):
                                ins = act.activation(prob[:, m % 4, TQ * q:TQ + T * q],
                                                     ps_s[m % 2][0:TQ, T * q:T * q + TQ * (q + 1)], ACT.Exp,
                                                     bias=maxes[:, m % 4, q:q + 1],
                                                     accum_out=sums[:, (m // GH) % 2, q, m % GH:m % GH + 1])
                            ins.then_inc(exp_done.sem, 1)
                        if name == "value":
                            act.wait_ge(o_psum, KT * b + (m + 1))
                            act.copy(rinv_T[:, m % 2], ps_o[m % 2][:, T:2 * T]).then_inc(rinvT_done, 1)
                        if kind == "last" and name == "score" and m == 10:
                            for u in range(2):
                                ws_next.round_hi(act, u)
                        if name not in ("T", "Q", "K", "V", "P", "R", "Y"):
                            continue
                        a = ps_acc[acc % 2]
                        act.wait_ge(acc_psum, acc0 + (acc + 1))
                        if name != "V":
                            f_free.wait_free(act, f0, f)
                        if name in ("T", "R"):
                            gain = (0 if name == "T" else 2) * KT + 2 * m
                            for k in range(2):
                                ins = act.activation(f_tile(name, f)[:, k], a[:, T * k:T * (k + 1)], ACT.Identity,
                                                     bias=cn["columns"][:, gain + KT + k:gain + KT + k + 1],
                                                     scale=cn["columns"][:, gain + k:gain + k + 1])
                        elif name in ("Q", "Y"):
                            ins = act.mul(f_tile(name, f), a[:, 0:T], SCALE)
                        elif name == "K":
                            ins = act.copy(f_tile(name, f), a[:, 0:T])
                        else:
                            ins = act.copy(f_tile(name, f) if name == "P" else v[:, m], a[0:TQ, :])
                        ins.then_inc(acc_read.sem, 1)

                plans.run(act, step)

            @block.vector
            def _(dve):
                dve.sem_inc(probT_done.sem, 2)
                dve.sem_inc(of_done.sem, 2)
                dve.sem_inc(olo_done.sem, 2)
                dve.tensor_copy(ident_r[:], cn["ident"][0:TQ, 0:TQ]).then_inc(ident_rounded, 1)

                def build_masks(b):
                    dve.wait_ge(mask_landed, 16 * b + 16)
                    dve.tensor_scalar(mask_f[:], mask_u8[:], MASKED, None, ALU.mult).then_inc(mask_ready, 1)
                    dve.wait_ge(mask_ready, b + 1)
                    for q in range(2):
                        ins = dve.tensor_tensor(masks[:, q], causal[:, q], mask_f[:], ALU.add)
                    ins.then_inc(masks_ready, 1)

                def token_statistics(b):
                    dve.wait_ge(x_landed, 16 * b + 16)
                    for t in range(2):
                        ln1.statistics(dve, t, xin[:, t])
                    ln1.variance(dve, b)

                def normalise_tokens(b):
                    for t in range(2):
                        ln1.normalise(dve, b, t, xin[:, t], xhat[:, t])

                def normalise_result(b):
                    for t in range(2):
                        ln2.normalise(dve, b, t, res[:, t], rhat[:, t])

                def finish_result(b):
                    dve.wait_ge(fin_landed, 16 * b + 16)
                    dve.tensor_tensor(fin[:], res[:], fin[:], ALU.add).then_inc(fin_done, 1)

                def step(kind, b, items):
                    acc0, f0, _, t0 = bases(kind, b)
                    if kind == "body0":
                        for u in range(6, len(units)):
                            ws.keep_lo(dve, u)
                    if kind == "first":
                        token_statistics(0)
                        normalise_tokens(0)
                        dve.wait_ge(bias_landed, 16)
                    if kind == "final":
                        normalise_result(b + -1)
                        finish_result(b + -1)
                    for name, ids, acc, f, _, s in items:
                        m = ids[0]
                        if kind == "first" and (name, m) in weights_before:
                            for u in weights_before[name, m]:
                                ws.keep_lo(dve, u)
                        if kind == "first" and (name, m) == ("Q", 3):
                            dve.wait_ge(causal_ready, 2)
                            build_masks(0)
                        if name == "score":
                            dve.wait_ge(s_psum, 16 * b + (m + 1))
                            dve.tensor_reduce(maxes[:, m % 4], ps_s[m % 2][0:TQ, 0:2 * T].rearrange(
                                "p (q t) -> p q t", q=2), AX_X, ALU.max, negate=True).then_inc(max_done, 1)
                            if kind != "body0" and m == 0:
                                normalise_result(b + -1)
                            if kind != "last" and m == 0:
                                token_statistics(b + 1)
                            if kind != "last" and m == 1:
                                normalise_tokens(b + 1)
                            if kind != "body0" and m == 2:
                                finish_result(b + -1)
                            if m == 8:
                                dve.wait_ge(res_landed, 16 * b + 16)
                                for t in range(2):
                                    dve.tensor_tensor(res[:, t], res[:, t], bias[:], ALU.add).then_inc(bias_added, 1)
                            if kind == "last" and m == 10:
                                for u in range(2):
                                    ws_next.keep_lo(dve, u)
                        if name == "probT" and m % GH == GH - 2:
                            g = m // GH
                            dve.wait_ge(exp_done.sem, exp_done.done(16 * b + (GH * g + GH - 1)))
                            dve.reciprocal(inv[:], sums[:, g % 2]).then_inc(inv_done, 1)
                            dve.wait_ge(inv_done, KT * b + (g + 1))
                            dve.tensor_copy(rinv[:, g % 2].rearrange("p q (j d) -> p q j d", d=HD),
                                            inv[:].unsqueeze(3).to_broadcast([TQ, 2, GH, HD])).then_inc(recip_done, 1)
                        if name == "probT":
                            dve.wait_ge(t_psum, 16 * b + (m + 1))
                            dve.tensor_copy(probT[0:TQ, m % 8], ps_t[m % 2][0:TQ, 0:T + TQ])\
                                .then_inc(probT_done.sem, 1)
                            if m == 15 and kind in ("body0", "body"):
                                build_masks(b + 1)
                        if name == "scale":
                            dve.wait_ge(rinvT_done, KT * b + (m + 1))
                            dve.wait_ge(olo_done.sem, olo_done.free(KT * b + m))
                            dve.tensor_tensor(of[:, m % 2], ps_o[m % 2][:, 0:T], rinv_T[:, m % 2], ALU.mult)\
                                .then_inc(of_done.sem, 1)
                            dve.wait_ge(of_done.sem, of_done.done(KT * b + m))
                            dve.tensor_copy(oT[:, HI, m], of[:, m % 2]).then_inc(ohi_done, 1)
                            dve.wait_ge(ohi_done, KT * b + (m + 1))
                            dve.tensor_tensor(oT[:, LO, m], of[:, m % 2], oT[:, HI, m].bitcast(F32),
                                              ALU.subtract).then_inc(olo_done.sem, 1)
                        if name == "split":
                            what, m = ids
                            dve.wait_ge(acc_read.sem, acc_read.done(acc0 + acc))
                            hi, src = split_dst(what, m, HI), f_tile(what, f)
                            dve.tensor_copy(hi, src).then_inc(thi_done, 1)
                            dve.wait_ge(thi_done, t0 + (s + 1))
                            dve.tensor_tensor(split_dst(what, m, LO), src, hi.bitcast(F32), ALU.subtract)\
                                .then_inc(f_free.sem(f), 1)
                        if name == "P":
                            dve.wait_ge(bias_added, 2 * b + 2)
                            dve.wait_ge(acc_read.sem, acc_read.done(acc0 + acc))
                            dve.tensor_tensor(res[:, m], f_tile(name, f), res[:, m], ALU.add)\
                                .then_inc(f_free.sem(f), 1)
                            f_free.wait_done(dve, f0, f)
                            ln2.statistics(dve, m, res[:, m])
                            if m == 1:
                                ln2.variance(dve, b)

                plans.run(dve, step)

            @block.tensor
            def _(pe):
                def step(kind, b, items):
                    acc0, f0, _, _ = bases(kind, b)
                    use = {(i[0], *i[1]): i[3] for i in items}
                    if kind == "first":
                        pe.wait_ge(ident_rounded, 1)
                    for name, ids, acc, f, _, _ in items:
                        m = ids[0]
                        if name == "score":
                            if m % 8 == 0:
                                pe.wait_ge(stacked[m // 8], STACKED * b + STACKED)
                            if m == 0:
                                pe.wait_ge(masks_ready, b + 1)
                            pe.wait_ge(exp_done.sem, exp_done.free(16 * b + m))
                            pe.matmul(ps_s[m % 2][0:TQ, 0:2 * T], ident_r[:], masks[:].rearrange("p q t -> p (q t)"),
                                      start=True, stop=False)
                            for q in range(2):
                                mm = pe.matmul(ps_s[m % 2][0:TQ, T * q:T * q + TQ * (q + 1)],
                                               q_stack[:, m, TQ * q:TQ * (q + 1)], k_stack[:, m, 0:TQ * (q + 1)],
                                               start=False, stop=q == 1)
                            mm.then_inc(s_psum, 1)
                        if name == "probT":
                            pe.wait_ge(exp_done.sem, exp_done.done(16 * b + m))
                            pe.wait_ge(probT_done.sem, probT_done.free(16 * b + m))
                            t, id_q = ps_t[m % 2], cn["ident"][0:TQ, 0:TQ]
                            for n in range(3):
                                mm = pe.transpose(t[0:TQ, TQ * n:TQ * (n + 1)], prob[:, m % 4, TQ * n:TQ * (n + 1)], id_q)
                            mm.then_inc(t_psum, 1)
                        if name == "value":
                            o = ps_o[m % 2]
                            pe.wait_ge(of_done.sem, of_done.free(KT * b + m))
                            pe.wait_ge(recip_done, KT * b + (m + 1))
                            for q in range(2):
                                pe.transpose(o[:, T + TQ * q:T + TQ * (q + 1)], rinv[:, m % 2, q, :],
                                             cn["ident"][0:TQ, 0:TQ])
                            if m == 0:
                                v1 = next(i[2] for i in items if i[:2] == ("V", (1,)))
                                pe.wait_ge(acc_read.sem, acc_read.done(acc0 + v1))
                            pe.wait_ge(probT_done.sem, probT_done.done(16 * b + (GH * m + GH - 1)))
                            for kt, cols in ((0, slice(0, T)), (1, slice(TQ, T))):
                                for j in range(GH):
                                    h = GH * m + j
                                    src = probT[0:TQ, h % 8, 0:T] if kt == 0 else probT[0:TQ, h % 8, T:T + TQ]
                                    mm = pe.matmul(o[HD * j:HD * (j + 1), cols], v[:, kt, HD * h:HD * (h + 1)], src,
                                                   start=kt == 0, stop=kt == 1)
                            mm.then_inc(o_psum, 1)
                        if name not in ("T", "Q", "K", "V", "P", "R", "Y"):
                            continue
                        a = ps_acc[acc % 2]
                        pe.wait_ge(acc_read.sem, acc_read.free(acc0 + acc))
                        if name in ("T", "R"):
                            src = xhat if name == "T" else rhat
                            if m == 0 and name == "T":
                                pe.wait_ge(ln1.xhat_done, 2 * b + 4)
                            if m == 0 and name == "R":
                                pe.wait_ge(ln2.xhat_done, 2 * b)
                            for k in range(2):
                                for t in range(2):
                                    mm = pe.transpose(a[:, T * k + TQ * t:T * k + TQ * (t + 1)],
                                                      src[:, t, P * (2 * m + k):P * (2 * m + k + 1)],
                                                      cn["ident"][0:TQ, 0:TQ])
                        elif name in ("Q", "K", "Y"):
                            src, wt = (rT, w["y"]) if name == "Y" else (xT, w[name.lower()])
                            if m == 0 and name != "K":
                                f_free.wait_done(pe, f0, use["R" if name == "Y" else "T", 1])
                            if kind == "first" and (name, m) == ("Q", 0):
                                pe.wait_ge(ws.lo_done, 2)
                            if kind == "first" and (name, m) == ("K", 0):
                                pe.wait_ge(ws.lo_done, 4)
                            if kind == "body" and (name, m) == ("Y", 0):
                                pe.wait_ge(ws.lo_done, 10)
                            mm = product(pe, a[:, 0:T], lambda c, k: wt[:, c, k, P * m:P * (m + 1)],
                                         lambda c, k: src[:, c, k, :])
                        else:
                            src, wt = (xT, w["v"]) if name == "V" else (oT, w["p"])
                            if (kind, name, m) in (("first", "V", 0), ("body0", "P", 0)):
                                pe.wait_ge(ws.lo_done, 6 if name == "V" else 8)
                            if name == "P" and m == 0:
                                pe.wait_ge(olo_done.sem, olo_done.done(KT * b + KT - 1))
                            mm = product(pe, a[0:TQ, :], lambda c, k: src[:, c, k, TQ * m:TQ * (m + 1)],
                                         lambda c, k: wt[:, c, k, :])
                        mm.then_inc(acc_psum, 1)

                plans.run(pe, step)


def plan_cross_attention(kind):
    ahead = [("T", k, a) for k in range(4) for a in range(2)]

    def keys(m, batches_ahead):
        return [("K", m, a, batches_ahead) for a in range(2)]

    if kind == "first":
        return ahead + keys(0, 1) + [("V", t) for t in range(4)]
    fill = {i: [("V", i)] for i in range(4 if kind == "body0" else 0, 6)}

    def put(tile_items, steps):
        for t, i in zip(tile_items, steps):
            fill.setdefault(i, []).append(t)

    if kind == "body0":
        put(keys(1, 0), (0, 1))
        put(keys(2, 0), (6, 7))
        put(keys(3, 0), (12, 13))
        put(ahead, range(14, 22))
        put(keys(0, 1) + keys(1, 1) + keys(2, 1), (22, 23, 27, 28, 32, 33))
    else:
        put(keys(3, 0), (6, 7))
    if kind == "body":
        put(ahead, range(8, 16))
        put(keys(0, 1) + keys(1, 1) + keys(2, 1), (17, 19, 22, 24, 28, 30))
    items, late = [], []
    for i in range(36):
        if i < 32:
            items.append(("score", i))
        if 3 <= i < 35:
            items.append(("probT", i - 3))
        if i < 32:
            items.append(("exp", i))
        items += late
        late = []
        if i >= 7 and i % 4 == 3:
            if i == 35:
                items.append(("E", 0))
            items.append(("value", (i - 7) // 4))
            late.append(("scale", (i - 7) // 4))
        items += fill.get(i, [])
    return items + late + [("E", 1)]


def cross_attention(nc, top, cn, w_first, ctx_tile, ctx_landed, ctx_in, ed_wkv, ed_wproj, res_out, q2_out, out):
    B, T, C = out.shape
    J = ctx_in.shape[1]
    KT = C // P
    H, HD, GH = 16, 32, 4
    TQ = T // 2
    NT = CTX_TILES
    JT = J // NT
    JH = J // 2
    JP = JH + 1
    STACK_Q, STACK_K = (HI, LO, HI), (HI, HI, LO)
    KS = 3 * HD
    STACKED_K, STACKED_Q = 16 * 3 * GH, 16 * 3
    SC, UN = 32, 8

    with ExitStack() as ph:
        def sem(name):
            return top.enter_context(nc.semaphore("ca_" + name))

        def sb(name, shape, dt):
            return ph.enter_context(nc.sbuf_tensor("ca_" + name, shape, dt))

        def pb(name, shape):
            return ph.enter_context(nc.psum_tensor("ca_" + name, shape, F32))

        wk = w_first
        wv = sb("wv", [P, 2, KT, C], F32R)
        wp = sb("wp", [P, KT, C], F32)
        xs = ctx_tile[0:JT]
        xT = sb("xT", [P, 2, KT, 2, JP], F32R)
        f32 = sb("f32", [P, 2, C], F32)
        keys = sb("keys", [P, 2, 2, JP], F32R)
        k_stack = sb("k_stack", [KS, H, 2, JP], F32R)
        q_stack = sb("q_stack", [KS, H, T], F32R)
        v = sb("v", [JT, NT, C], F32)
        prob = sb("prob", [TQ, 4, 2, JH], F32)
        probT = sb("probT", [P, 2, GH, NT, TQ], F32)
        maxes = sb("maxes", [TQ, 4], F32)
        sums = sb("sums", [TQ, 2, GH], F32)
        inv = sb("inv", [TQ, GH], F32)
        rinv = sb("rinv", [TQ, P], F32)
        rinv_T = sb("rinv_T", [P, TQ], F32)
        oT = sb("oT", [P, KT, T], F32)
        res = sb("res", [TQ, 2, C], F32)
        ps_s = [pb(f"ps_s{i}", [P, 2, 512]) for i in range(2)]
        ps_t = [pb(f"ps_t{i}", [P, 512]) for i in range(2)]
        ps_o = pb("ps_o", [P, 512])
        ps_acc = pb("ps_acc", [P, 512])

        ln = LayerNorm("ca_ln", lambda n: top.enter_context(nc.semaphore(n)), sb, JT, NT, cn["neg_half"])
        res_landed, wp_landed = sem("res_landed"), sem("wp_landed")
        k_stacked = [sem(f"k_stacked{m}") for m in range(KT)]
        q_stacked = [sem(f"q_stacked{i}") for i in range(2)]
        pad_zeroed = sem("pad_zeroed")
        s_psum, max_done = sem("s_psum"), sem("max_done")
        exp_done = Count(sem("exp_done"), primed=2)
        t_psum = [sem(f"t_psum{i}") for i in range(2)]
        pt_done = [Count(sem(f"pt_done{i}"), primed=1) for i in range(2)]
        inv_done, rinv_done, rinvT_done, o_psum = (sem(n) for n in ("inv_done", "rinv_done", "rinvT_done", "o_psum"))
        o_done = Count(sem("o_done"), primed=1)
        acc_psum, hi_done = sem("acc_psum"), sem("hi_done")
        acc_read = Count(sem("acc_read"), primed=1)
        f_free = TwoTiles([sem(f"f_free{i}") for i in range(2)])
        out_stored = Count(sem("out_stored"), unit=16, primed=1)

        stage_t = probT[:].rearrange("p a b c d -> p (a b c d)")
        stage = [stage_t[:, 2 * C * i:2 * C * (i + 1)].rearrange("p (k n) -> p k n", k=2) for i in range(2)]
        ws = WeightSplitter(weight_halves(ed_wkv[:, C:2 * C], wv), stage, [sem(f"w_landed{i}") for i in range(2)],
                            sem("w_hi"), sem("w_lo"))
        plans = Plans(plan_cross_attention, B, ("first", "body0", "body", "last"))
        bases = plans.bases

        def f_tile(name, f):
            if name == "E":
                return f32[0:TQ, f % 2, :]
            return f32[:, f % 2, 0:JP if name == "K" else JH]

        def split_dst(name, m, a, half):
            return xT[:, half, m, a, 0:JH] if name == "T" else keys[:, half, a, :]

        with nc.Block() as block:
            @block.sync
            def _(sp):
                sp.sem_inc(out_stored.sem, 16)
                ctx_tokens = lambda b: ctx_in[b].rearrange("(p t) c -> p t c", t=NT)
                tokens = lambda a, b: a[b].rearrange("(t p) c -> p t c", p=TQ)
                ws.load(sp)
                sp.dma_start(wp[:], ed_wproj.rearrange("(k p) n -> p k n", p=P)).then_inc(wp_landed, 16)

                def stack_queries(pair, b):
                    for c, half in enumerate(STACK_Q):
                        sp.dma_start(q_stack[HD * c:HD * (c + 1), 8 * pair:8 * pair + 8, :].bitcast(F32),
                                     q2_out[b, half, 2 * pair:2 * pair + 2].rearrange(
                                         "k (j d) t -> d (k j) t", d=HD)).then_inc(q_stacked[pair], 16)

                def stack_keys(m):
                    for j in range(GH):
                        for c, half in enumerate(STACK_K):
                            sp.dma_start(k_stack[HD * c:HD * (c + 1), GH * m + j].bitcast(F32),
                                         keys[HD * j:HD * (j + 1), half].bitcast(F32)).then_inc(k_stacked[m], 16)

                def step(kind, b, items, next_x=True):
                    acc0, f0, _, _ = bases(kind, b)
                    if kind == "first":
                        stack_queries(0, 0)
                        stack_queries(1, 0)
                    else:
                        sp.wait_ge(out_stored.sem, out_stored.free(b))
                        sp.dma_start(res[:], tokens(res_out, b)).then_inc(res_landed, 16)
                    for name, ids, acc, f, _, _ in items:
                        if name == "T" and ids == (KT - 1, 1) and next_x:
                            sp.wait_ge(acc_psum, acc0 + (acc + 1))
                            sp.dma_start(xs[:], ctx_tokens(b + 2)).then_inc(ctx_landed, 16)
                        if name == "K" and ids[1] == 1:
                            f_free.wait_done(sp, f0, f)
                            stack_keys(ids[0])
                        if name == "score" and ids[0] % 16 == 15 and kind != "last":
                            sp.wait_ge(s_psum, SC * b + (ids[0] + 1))
                            stack_queries(ids[0] // 16, b + 1)
                        if name == "E" and ids[0] == 1:
                            f_free.wait_done(sp, f0, f)
                            sp.dma_start(tokens(out, b), res[:]).then_inc(out_stored.sem, 16)

                step("first", -1, plans.items["first"])
                step("body0", 0, plans.items["body0"])
                with sp.Fori(1, B - 2) as b:
                    step("body", b, plans.items["body"])
                step("body", B - 2, plans.items["body"], next_x=False)
                step("last", B - 1, plans.items["last"], next_x=False)
                sp.wait_ge(out_stored.sem, out_stored.done(B - 1))

            @block.gpsimd
            def _(pool):
                for tile in range(2):
                    pool.sem_inc(f_free.sems[tile], 1)
                pool.memset(xT[:].bitcast(F32), 0.0).then_inc(pad_zeroed, 1)

                def step(kind, b, items):
                    acc0, f0, sp0, t0 = bases(kind, b)
                    if kind != "last":
                        ln.inverse_root(pool, b + 1)
                    for name, ids, acc, f, s, t in items:
                        if name in ("T", "K"):
                            m, a = ids[:2]
                            pool.wait_ge(acc_read.sem, acc_read.done(acc0 + acc))
                            if name == "K" and a == 0 and (kind, m) != ("first", 0):
                                pool.wait_ge(k_stacked[(m - 1) % KT], STACKED_K * (b + (1 + ids[2] - (m == 0))))
                            split_exactly(pool, cn["one"], split_dst(name, m, a, HI), split_dst(name, m, a, LO),
                                          f_tile(name, f), hi_done, (sp0 + t0) + (s + t + 1)).then_inc(f_free.sem(f), 1)
                        if name == "E":
                            if ids[0] == 0:
                                pool.wait_ge(res_landed, 16 * b + 16)
                            pool.wait_ge(acc_read.sem, acc_read.done(acc0 + acc))
                            pool.tensor_tensor(res[:, ids[0]], f_tile(name, f), res[:, ids[0]], ALU.add)\
                                .then_inc(f_free.sem(f), 1)

                plans.run(pool, step)

            @block.scalar
            def _(act):
                act.sem_inc(exp_done.sem, 2)
                act.sem_inc(pt_done[0].sem, 1)
                act.sem_inc(acc_read.sem, 1)

                def step(kind, b, items):
                    acc0, f0, _, _ = bases(kind, b)
                    if kind == "first":
                        for u in range(2):
                            ws.round_hi(act, u)
                    for name, ids, acc, f, _, _ in items:
                        m = ids[0]
                        if name == "exp":
                            act.wait_ge(max_done, SC * b + (m + 1))
                            act.activation(prob[:, m % 4], ps_s[m % 2][0:TQ, :, 0:JH], ACT.Exp,
                                           bias=maxes[:, m % 4:m % 4 + 1],
                                           accum_out=sums[:, (m // GH) % 2, m % GH:m % GH + 1])\
                                .then_inc(exp_done.sem, 1)
                        if name == "probT":
                            act.wait_ge(t_psum[0], SC * b + (m + 1))
                            act.copy(probT[0:JT, (m // GH) % 2, m % GH, 0:3],
                                     ps_t[0][0:JT, 0:3 * TQ].rearrange("p (t q) -> p t q", q=TQ))\
                                .then_inc(pt_done[0].sem, 1)
                        if name not in ("V", "K", "T", "E"):
                            continue
                        act.wait_ge(acc_psum, acc0 + (acc + 1))
                        if name != "V":
                            f_free.wait_free(act, f0, f)
                        if name == "T":
                            ins = act.activation(f_tile(name, f), ps_acc[:, 0:JH], ACT.Identity,
                                                 bias=cn["columns"][:, 3 * KT + m:3 * KT + m + 1],
                                                 scale=cn["columns"][:, 2 * KT + m:2 * KT + m + 1])
                        elif name == "K":
                            ins = act.copy(f_tile(name, f), ps_acc[:, 0:JP])
                        elif name == "V":
                            ins = act.copy(v[:, m], ps_acc[0:JT, :])
                        else:
                            ins = act.copy(f_tile(name, f), ps_acc[0:TQ, :])
                        ins.then_inc(acc_read.sem, 1)

                plans.run(act, step)

            @block.vector
            def _(dve):
                dve.sem_inc(pt_done[1].sem, 1)
                dve.sem_inc(o_done.sem, 1)

                def statistics(b, tiles):
                    if tiles[0] == 0:
                        dve.wait_ge(ctx_landed, 16 * b + 16)
                    for t in tiles:
                        ln.statistics(dve, t, xs[:, t])
                    if tiles[-1] == NT - 1:
                        ln.variance(dve, b)

                def normalise(b, tiles):
                    for t in tiles:
                        ln.normalise(dve, b, t, xs[:, t], xs[:, t])

                def step(kind, b, items):
                    acc0, _, _, _ = bases(kind, b)
                    if kind == "first":
                        statistics(0, range(NT))
                        normalise(0, range(NT))
                        for u in range(2):
                            ws.keep_lo(dve, u)
                    for name, ids, acc, f, _, _ in items:
                        m = ids[0]
                        if name == "score":
                            dve.wait_ge(s_psum, SC * b + (m + 1))
                            dve.tensor_reduce(maxes[:, m % 4:m % 4 + 1], ps_s[m % 2][0:TQ, :, 0:JH],
                                              mybir.AxisListType.XY, ALU.max, negate=True).then_inc(max_done, 1)
                            if kind != "last" and m < 3:
                                statistics(b + 1, range(2 * m, 2 * m + 2))
                            if kind != "last" and 4 <= m < 7:
                                normalise(b + 1, range(2 * m - 8, 2 * m - 6))
                        if name == "probT":
                            u = m // GH
                            if m % GH == 1:
                                dve.wait_ge(exp_done.sem, exp_done.done(SC * b + (GH * u + GH - 1)))
                                dve.reciprocal(inv[:], sums[:, u % 2]).then_inc(inv_done, 1)
                                dve.wait_ge(inv_done, UN * b + (u + 1))
                                dve.tensor_copy(rinv[:].rearrange("p (j d) -> p j d", d=HD),
                                                inv[:].unsqueeze(2).to_broadcast([TQ, GH, HD])).then_inc(rinv_done, 1)
                            dve.wait_ge(t_psum[1], SC * b + (m + 1))
                            if m % GH == GH - 1:
                                dve.tensor_copy(rinv_T[:], ps_t[1][:, 3 * TQ:4 * TQ]).then_inc(rinvT_done, 1)
                            dve.tensor_copy(probT[0:JT, u % 2, m % GH, 3:6],
                                            ps_t[1][0:JT, 0:3 * TQ].rearrange("p (t q) -> p t q", q=TQ))\
                                .then_inc(pt_done[1].sem, 1)
                        if name == "scale":
                            q = m % 2
                            dve.wait_ge(o_psum, UN * b + (m + 1))
                            dve.wait_ge(rinvT_done, UN * b + (m + 1))
                            dve.tensor_tensor(oT[:, m // 2, TQ * q:TQ * (q + 1)], ps_o[:, TQ * q:TQ * (q + 1)],
                                              rinv_T[:], ALU.mult).then_inc(o_done.sem, 1)

                plans.run(dve, step)

            @block.tensor
            def _(pe):
                ident = cn["ident"]

                def step(kind, b, items):
                    acc0, f0, _, _ = bases(kind, b)
                    for name, ids, acc, f, _, _ in items:
                        m = ids[0]
                        if name == "score":
                            g, q, h = m // 8, (m // GH) % 2, GH * (m // 8) + m % GH
                            if m % 8 == 0:
                                pe.wait_ge(k_stacked[g], STACKED_K * b + STACKED_K)
                            if m % 16 == 0:
                                pe.wait_ge(q_stacked[m // 16], STACKED_Q * b + STACKED_Q)
                            pe.wait_ge(exp_done.sem, exp_done.free(SC * b + m))
                            for a in range(2):
                                mm = pe.matmul(ps_s[m % 2][0:TQ, a, 0:JP], q_stack[:, h, TQ * q:TQ * (q + 1)],
                                               k_stack[:, h, a, :], start=True, stop=True)
                            mm.then_inc(s_psum, 1)
                        if name == "probT":
                            pe.wait_ge(exp_done.sem, exp_done.done(SC * b + m))
                            for a in range(2):
                                pe.wait_ge(pt_done[a].sem, pt_done[a].free(SC * b + m))
                                if a == 1 and m % GH == GH - 1:
                                    pe.wait_ge(rinv_done, UN * b + (m // GH + 1))
                                    pe.transpose(ps_t[1][:, 3 * TQ:4 * TQ], rinv[:], ident[0:TQ, 0:TQ])
                                for t in range(3):
                                    mm = pe.transpose(ps_t[a][0:JT, TQ * t:TQ * (t + 1)],
                                                      prob[:, m % 4, a, JT * t:JT * (t + 1)], ident[0:TQ, 0:TQ])
                                mm.then_inc(t_psum[a], 1)
                        if name == "value":
                            g, q = m // 2, m % 2
                            if m == 0:
                                last_v = max(i[2] for i in items if i[0] == "V")
                                pe.wait_ge(acc_read.sem, acc_read.done(acc0 + last_v))
                            for a in range(2):
                                pe.wait_ge(pt_done[a].sem, pt_done[a].done(SC * b + (GH * m + GH - 1)))
                            pe.wait_ge(o_done.sem, o_done.free(UN * b + m))
                            for t in range(NT):
                                for j in range(GH):
                                    h = GH * g + j
                                    mm = pe.matmul(ps_o[HD * j:HD * (j + 1), TQ * q:TQ * (q + 1)],
                                                   v[:, t, HD * h:HD * (h + 1)], probT[0:JT, m % 2, j, t],
                                                   start=t == 0, stop=t == NT - 1)
                            mm.then_inc(o_psum, 1)
                        if name not in ("V", "K", "T", "E"):
                            continue
                        pe.wait_ge(acc_read.sem, acc_read.free(acc0 + acc))
                        if name == "T":
                            a = ids[1]
                            if m == 0 and a == 0:
                                pe.wait_ge(ln.xhat_done, NT * b + 2 * NT)
                            for t in range(3):
                                mm = pe.transpose(ps_acc[:, JT * t:JT * (t + 1)], xs[:, 3 * a + t, P * m:P * (m + 1)],
                                                  ident[0:JT, 0:JT])
                        elif name == "K":
                            a = ids[1]
                            if m == 0 and a == 0:
                                last_t = max(i[3] for i in items if i[0] == "T")
                                f_free.wait_done(pe, f0, last_t)
                                if kind == "first":
                                    pe.wait_ge(pad_zeroed, 1)
                            mm = product(pe, ps_acc[:, 0:JP], lambda c, k: wk[:, c, k, P * m:P * (m + 1)],
                                         lambda c, k: xT[:, c, k, a, :])
                        elif name == "V":
                            a, t = m // 3, m % 3
                            if kind == "first" and m == 0:
                                pe.wait_ge(ws.lo_done, 2)
                            mm = product(pe, ps_acc[0:JT, :], lambda c, k: xT[:, c, k, a, JT * t:JT * (t + 1)],
                                         lambda c, k: wv[:, c, k, :])
                        else:
                            pe.wait_ge(o_done.sem, o_done.done(UN * b + (6 + m)))
                            for g in range(KT):
                                mm = pe.matmul(ps_acc[0:TQ, :], oT[:, g, TQ * m:TQ * (m + 1)], wp[:, g, :],
                                               start=g == 0, stop=g == KT - 1)
                        mm.then_inc(acc_psum, 1)
                    if kind == "first":
                        pe.wait_ge(wp_landed, 16)

                plans.run(pe, step)


_PRE = "L0_xattn_"
_INS = ["x", "ctx_1024", "mask_BxS_bf0"] + [_PRE + n for n in (
    "sa_wqkv", "sa_wproj", "sa_bproj", "ed_wkv", "ed_wq", "ed_wproj", "ed_bproj", "ff_w1", "ff_b1", "ff_w2", "ff_b2",
    "ln1_g", "ln1_b", "ln2_g", "ln2_b", "ln3_g", "ln3_b")]


def kernel(**inputs):
    import numpy as _np
    import concourse.bacc as _bacc
    from concourse import mybir as _mybir
    from concourse.bass_utils import run_bass_kernel_spmd as _run

    nc = _bacc.Bacc("TRN2", target_bir_lowering=False, num_devices=1)
    arrays, args = {}, []
    for name in _INS:
        a = _np.ascontiguousarray(inputs[name])
        arrays[f"in_{name}_dram"] = a
        args.append(nc.dram_tensor(f"in_{name}_dram", a.shape, _mybir.dt.from_np(a.dtype), kind="ExternalInput").ap())
    out = nc.dram_tensor("out_0_dram", inputs["x"].shape, _mybir.dt.float32, kind="ExternalOutput").ap()
    xattn_kernel(nc, *args, out)
    r = _run(nc, [arrays], core_ids=[0])
    return r.results[0]["out_0_dram"]
```
